# Optimizing a Trainium2 kernel written in Bass

```python
import numpy as np
import jax
import jax.numpy as jnp

def _softmax(x, axis=-1):
    return jax.nn.softmax(x, axis=axis)

def _gelu(x):
    return jax.nn.gelu(x, approximate=True)

def _silu(x):
    return jax.nn.silu(x)

def _sigmoid(x):
    return jax.nn.sigmoid(x)

def _layernorm(x, axis=-1, eps=1e-05):
    m = jnp.mean(x, axis=axis, keepdims=True)
    v = jnp.var(x, axis=axis, keepdims=True)
    return (x - m) / jnp.sqrt(v + eps)

def _scatter_add(tgt, idx, src, axis=0):
    return tgt.at[idx].add(src)

def _segment_sum(src, seg, n):
    return jax.ops.segment_sum(src, seg, n)
kernel_name = 'mk_adj_ffn_d1_adj_r2_ceccd5'

def setup_inputs(seed: int=0):
    np.random.seed(seed)
    _w = jnp.asarray

    def _rec_inputs():
        import jax
        import jax.numpy as jnp
        _gk = jax.random.key(seed)
        x = -0.0002928 + 1 * jax.random.normal(jax.random.fold_in(_gk, 1), (16, 512, 128), jnp.float32)
        _a = jax.random.bernoulli(jax.random.fold_in(_gk, 2), 0.03125, (16, 512, 512))
        _a = jnp.logical_or(_a, jnp.swapaxes(_a, -1, -2))
        _a = jnp.logical_or(_a, jnp.eye(512, dtype=bool))
        _af = _a.astype(jnp.float32)
        _af = _af * jax.random.uniform(jax.random.fold_in(_gk, 3), (16, 512, 512), jnp.float32, 0.05, 1)
        adj = _af
        return (x, adj)
    x, adj = _rec_inputs()

    def _L0_gnn_setup():
        import jax, jax.numpy as jnp
        import numpy as np
        key = jax.random.key(seed)
        k1, k2, k3, k4 = jax.random.split(key, 4)
        B, N, F_in, F_out = (8, 1024, 128, 128)
        x = jax.random.normal(k1, (B, N, F_in), dtype=jnp.float32)
        adj = jax.random.uniform(k2, (B, N, N), dtype=jnp.float32)
        stdv = 1.0 / np.sqrt(F_out)
        weight = jax.random.uniform(k3, (F_in, F_out), dtype=jnp.float32, minval=-stdv, maxval=stdv)
        bias = jax.random.uniform(k4, (F_out,), dtype=jnp.float32, minval=-stdv, maxval=stdv)
        return {'x': x, 'adj': adj, 'weight': weight, 'bias': bias}
    _L0_gnn_all = _L0_gnn_setup()
    _L0_gnn_in = {k: v for k, v in _L0_gnn_all.items() if k in ('weight', 'bias')}
    del _L0_gnn_all

    def _L0_ffn_setup():
        import jax, jax.numpy as jnp
        import numpy as np
        TOP_K = 2
        LN_EPS = 1e-05
        key = jax.random.key(seed)
        ks = jax.random.split(key, 8)
        B, S, D, E, H = (16, 512, 128, 8, 512)
        x = jax.random.normal(ks[0], (B, S, D), dtype=jnp.float32)
        Wr = jax.random.normal(ks[1], (D, E), dtype=jnp.float32) * 0.1
        br = jnp.zeros((E,), dtype=jnp.float32)
        ln_g = jnp.ones((E, D), dtype=jnp.float32)
        ln_b = jnp.zeros((E, D), dtype=jnp.float32)
        W1 = jax.random.normal(ks[2], (E, D, H), dtype=jnp.float32) * (1.0 / np.sqrt(D))
        b1 = jnp.zeros((E, H), dtype=jnp.float32)
        W2 = jax.random.normal(ks[3], (E, H, D), dtype=jnp.float32) * (1.0 / np.sqrt(H))
        b2 = jnp.zeros((E, D), dtype=jnp.float32)
        return {'x': x, 'Wr': Wr, 'br': br, 'ln_g': ln_g, 'ln_b': ln_b, 'W1': W1, 'b1': b1, 'W2': W2, 'b2': b2}
    _L0_ffn_all = _L0_ffn_setup()
    _L0_ffn_in = {k: v for k, v in _L0_ffn_all.items() if k in ('Wr', 'br', 'ln_g', 'ln_b', 'W1', 'b1', 'W2', 'b2')}
    del _L0_ffn_all
    return {'x': x, 'adj': adj, 'L0_gnn_weight': _L0_gnn_in['weight'], 'L0_gnn_bias': _L0_gnn_in['bias'], 'L0_ffn_Wr': _L0_ffn_in['Wr'], 'L0_ffn_br': _L0_ffn_in['br'], 'L0_ffn_ln_g': _L0_ffn_in['ln_g'], 'L0_ffn_ln_b': _L0_ffn_in['ln_b'], 'L0_ffn_W1': _L0_ffn_in['W1'], 'L0_ffn_b1': _L0_ffn_in['b1'], 'L0_ffn_W2': _L0_ffn_in['W2'], 'L0_ffn_b2': _L0_ffn_in['b2']}

def reference(x, adj, L0_gnn_weight, L0_gnn_bias, L0_ffn_Wr, L0_ffn_br, L0_ffn_ln_g, L0_ffn_ln_b, L0_ffn_W1, L0_ffn_b1, L0_ffn_W2, L0_ffn_b2):
    import jax
    import jax.numpy as jnp

    def _L0_gnn_ref(x, adj, weight, bias):
        import jax, jax.numpy as jnp
        import numpy as np
        support = jnp.einsum('bni,io->bno', x, weight)
        out = jnp.einsum('bnm,bmo->bno', adj, support)
        return out + bias

    def _L0_ffn_ref(x, Wr, br, ln_g, ln_b, W1, b1, W2, b2):
        import jax, jax.numpy as jnp
        import numpy as np
        TOP_K = 2
        LN_EPS = 1e-05
        B, S, D = x.shape
        N = B * S
        xt = x.reshape(N, D)
        logits = xt @ Wr + br
        probs = jax.nn.softmax(logits, axis=-1)
        top_p, top_idx = jax.lax.top_k(probs, TOP_K)
        weights = top_p / top_p.sum(axis=-1, keepdims=True)
        mu = xt.mean(axis=-1, keepdims=True)
        var = ((xt - mu) ** 2).mean(axis=-1, keepdims=True)
        xn = (xt - mu) * jax.lax.rsqrt(var + LN_EPS)
        xe = xn[None, :, :] * ln_g[:, None, :] + ln_b[:, None, :]
        h = jax.nn.gelu(jnp.einsum('end,edh->enh', xe, W1) + b1[:, None, :], approximate=False)
        y = jnp.einsum('enh,ehd->end', h, W2) + b2[:, None, :]
        y_tok = jnp.transpose(y, (1, 0, 2))
        sel = jnp.take_along_axis(y_tok, top_idx[:, :, None], axis=1)
        out = (weights[:, :, None] * sel).sum(axis=1)
        return out.reshape(B, S, D)
    x = x + _L0_gnn_ref(_layernorm(x, axis=-1), adj, L0_gnn_weight, L0_gnn_bias)
    x = x + _L0_ffn_ref(_layernorm(x, axis=-1), L0_ffn_Wr, L0_ffn_br, L0_ffn_ln_g, L0_ffn_ln_b, L0_ffn_W1, L0_ffn_b1, L0_ffn_W2, L0_ffn_b2)
    return x

_drawn_inputs = setup_inputs


def setup_inputs(seed=0):
    import zlib

    import numpy as np

    out = dict(_drawn_inputs(seed))
    spreads = {'L0_ffn_br': (0.0, 0.1),
     'L0_ffn_ln_g': (1.0, 0.2),
     'L0_ffn_ln_b': (0.0, 0.355),
     'L0_ffn_b1': (0.0, 0.357),
     'L0_ffn_b2': (0.0, 0.1)}
    factors = {}
    for name, (base, spread) in spreads.items():
        noise = np.random.default_rng([zlib.crc32(name.encode()), seed]).standard_normal(out[name].shape)
        drawn = base * np.exp(spread * noise) if base else spread * noise
        out[name] = jnp.asarray(drawn.astype(out[name].dtype))
    for name, factor in factors.items():
        out[name] = (out[name] * factor).astype(out[name].dtype)
    return out
```

```python
import concourse.bass as bass
from concourse import mybir
from contextlib import ExitStack

FP32 = mybir.dt.float32
BF16 = mybir.dt.bfloat16
I32 = mybir.dt.int32
ALU = mybir.AluOpType
ACT = mybir.ActivationFunctionType
AX = mybir.AxisListType

P = 128
LN_EPS = 1e-5
BIG = 3.0e38


def build(nc, x, adj, gnn_w, gnn_b, wr, br, ln_g, ln_b, w1, b1, w2, b2, out):
    B, N, D = x.shape
    E = wr.shape[1]
    H = w1.shape[2]
    Q = N // P
    HC = H // P
    K = 2
    TOK = B * N
    UNITS = B // 2
    UT = 2 * Q
    TILE = 2 * P
    TILES = TOK * K // TILE + E
    REGION = TOK + TILE
    DUMMY = E * REGION
    RW = D + 2
    NOWHERE = float(4 * TOK)
    WP = H + HC * D + D + HC
    O_W2, O_B2, O_B1 = H, H + HC * D, H + HC * D + D
    NS = 4
    MAXT = TOK // TILE

    ctx = ExitStack()
    with ctx:
        def sb(name, shape, dt=FP32):
            return ctx.enter_context(nc.sbuf_tensor(name, shape, dt))

        def sem(name):
            return ctx.enter_context(nc.semaphore(name))

        sorted_rows = nc.dram_tensor("sorted_rows", [DUMMY + TILE, RW], FP32, kind="Internal").ap()
        result_rows = nc.dram_tensor("result_rows", [TOK * K, D], FP32, kind="Internal").ap()

        ident = sb("ident", [P, P])
        before = sb("before", [P, P], BF16)
        ones = sb("ones", [P, P], BF16)
        ones_row = sb("ones_row", [1, P])
        prefer_low = sb("prefer_low", [P, E])
        region_of = sb("region_of", [P, E])
        iota_i = sb("iota_i", [P, 80], I32)
        bias_row = sb("bias_row", [1, Q, D])
        wg_sb = sb("wg_sb", [P, D])
        wr_sb = sb("wr_sb", [P, E])
        br_sb = sb("br_sb", [P, E])
        VR = E * HC + 2 * E
        vecs = sb("vecs", [VR, P])
        vecT = sb("vecT", [P, VR])
        gcol = vecT[:, E * HC:E * HC + E]
        bcol = vecT[:, E * HC + E:VR]
        minus_half = sb("minus_half", [P, UT])
        veps = sb("veps", [P, UT])
        pad_tile = sb("pad_tile", [P, 2, RW])

        x_all = sb("x_all", [P, B, Q, D])
        adj_sb = [sb(f"adj_sb{g}", [P, Q, N]) for g in range(2)]
        adjT = [sb(f"adjT{g}", [P, Q, N]) for g in range(2)]
        xn = [sb(f"xn{g}", [P, Q, D]) for g in range(2)]
        gT = [sb(f"gT{g}", [P, N]) for g in range(2)]
        z = [sb(f"z{g}", [P, Q, D]) for g in range(2)]
        zT = [sb(f"zT{g}", [P, N]) for g in range(2)]
        st1 = sb("st1", [P, UT, 6])
        st2 = sb("st2", [P, UT, 6])
        (d1, v1, s1, q1, var1, rstd1, nmr1,
         d2, v2, s2, q2, var2, rstd2, t2, u2, mean2, rstd3, scale3) = (
            sb(n, [P, UT]) for n in ("d1", "v1", "s1", "q1", "var1", "rstd1", "nmr1",
                                     "d2", "v2", "s2", "q2", "var2", "rstd2", "t2", "u2", "mean2", "rstd3", "scale3"))
        rows = [sb(f"rows{u}", [P, UT, K, RW]) for u in range(2)]
        slot = [sb(f"slot{u}", [P, K, UT], I32) for u in range(2)]
        lg = sb("lg", [P, UT, E])
        lg2 = sb("lg2", [P, UT, E])
        top1, top2, gap, key1, key2, e2, den = (
            sb(n, [P, UT]) for n in ("top1", "top2", "gap", "key1", "key2", "e2", "den"))
        eq1 = sb("eq1", [P, UT, E])
        eq2 = sb("eq2", [P, UT, E])
        kk1 = sb("kk1", [P, UT, E])
        kk2 = sb("kk2", [P, UT, E])
        onehot = sb("onehot", [P, K, UT, E])
        sel = sb("sel", [P, UT, E], BF16)
        pos = sb("pos", [P, UT, E])
        place = sb("place", [P, K, UT, E])
        sel_sum = sb("sel_sum", [P, E])
        sel_before = sb("sel_before", [P, E], BF16)

        cnt = sb("cnt", [1, E])
        thr = sb("thr", [1, MAXT])
        more = sb("more", [1, E, MAXT])
        nt = sb("nt", [1, E])
        one8 = sb("one8", [1, E])
        t_end = sb("t_end", [1, E])
        t_start = sb("t_start", [1, E])
        base_row = sb("base_row", [1, E])
        tnum = sb("tnum", [1, TILES])
        tnum8 = sb("tnum8", [1, TILES])
        ge_end = sb("ge_end", [1, TILES, E])
        ge_start = sb("ge_start", [1, TILES, E])
        mine = sb("mine", [1, TILES, E])
        mine_row = sb("mine_row", [1, TILES, E])
        eid = sb("eid", [1, TILES])
        real = sb("real", [1, TILES])
        row_a = sb("row_a", [1, TILES])
        row_b = sb("row_b", [1, TILES])
        tab_e = sb("tab_e", [1, TILES], I32)
        tab_row = sb("tab_row", [1, TILES], I32)
        tab_pad = sb("tab_pad", [1, E], I32)

        wpack = sb("wpack", [P, E, WP])
        wbuf = [sb(f"wbuf{s}", [P, WP]) for s in range(NS)]
        xt = [sb(f"xt{s}", [P, 2, RW]) for s in range(NS)]
        xT = [sb(f"xT{s}", [P, TILE]) for s in range(2)]
        hT = [sb(f"hT{s}", [P, HC, TILE]) for s in range(2)]
        yb = [sb(f"yb{s}", [P, 2, D]) for s in range(2)]
        ys = [sb(f"ys{s}", [P, 2, D]) for s in range(2)]

        y2 = [adj_sb[s // 2][:, 2 * (s % 2):2 * (s % 2) + 2, :].rearrange("p a n -> p (a n)")
              .rearrange("p (q c) -> p q c", q=Q) for s in range(NS)]
        fin = [adjT[s // 2][:, s % 2, :].rearrange("p (q d) -> p q d", q=Q) for s in range(NS)]

        bank = [ctx.enter_context(nc.psum_tensor(f"bank{i}", [P, 512], FP32)) for i in range(8)]
        psT = [bank[0], bank[1]]
        psG = bank[2]
        psO = [bank[3], bank[4]]
        psZ = [bank[5], bank[6]]
        psL = bank[7][:, 0:UT * E].rearrange("p (t e) -> p t e", e=E)
        psR = bank[7][:, UT * E:2 * UT * E].rearrange("p (t e) -> p t e", e=E)
        psCnt = bank[7][:, 2 * UT * E:2 * UT * E + E]
        psB1 = bank[7][:, 256:256 + E * HC]
        psVec = bank[7][:, 384:384 + VR]
        psH = [bank[c] for c in range(HC)]
        psX = bank[4]
        psY = [bank[5], bank[6]]

        x0_loaded = sem("x0_loaded")
        xrest_loaded = sem("xrest_loaded")
        small_loaded = sem("small_loaded")
        adj_loaded = [sem(f"adj_loaded{g}") for g in range(2)]
        weights_loaded = sem("weights_loaded")
        pool_const = sem("pool_const")
        dve_const = sem("dve_const")
        dummy_written = sem("dummy_written")
        ln1 = sem("ln1")
        rstd1_ready = sem("rstd1_ready")
        xn_ready = sem("xn_ready")
        adj_turned = sem("adj_turned")
        adjT_ready = sem("adjT_ready")
        g_done = sem("g_done")
        gT_ready = sem("gT_ready")
        w_done = sem("w_done")
        x1_ready = sem("x1_ready")
        ln2 = sem("ln2")
        rstd2_ready = sem("rstd2_ready")
        rstd3_ready = sem("rstd3_ready")
        z_turned = sem("z_turned")
        zT_ready = sem("zT_ready")
        l_done = sem("l_done")
        rows_ready = sem("rows_ready")
        route = sem("route")
        exp_ready = sem("exp_ready")
        rank_done = sem("rank_done")
        scattered = [sem(f"scattered{u}") for u in range(2)]
        counted = sem("counted")
        table = sem("table")
        pads_written = sem("pads_written")
        vecs_turned = sem("vecs_turned")
        vecT_ready = sem("vecT_ready")
        b1_done = sem("b1_done")
        w1_scaled = sem("w1_scaled")
        wpack_ready = sem("wpack_ready")
        xt_loaded = [sem(f"xt_loaded{s}") for s in range(NS)]
        wbuf_loaded = [sem(f"wbuf_loaded{s}") for s in range(NS)]
        xt_turned = sem("xt_turned")
        xT_ready = sem("xT_ready")
        h_done = sem("h_done")
        gelu_done = sem("gelu_done")
        y_done = sem("y_done")
        yb_ready = sem("yb_ready")
        ys_ready = sem("ys_ready")
        y_scattered = [sem(f"y_scattered{s}") for s in range(2)]
        y2_loaded = [sem(f"y2_loaded{s}") for s in range(NS)]
        sum1 = sem("sum1")
        sum2 = sem("sum2")
        stored = [sem(f"stored{s}") for s in range(NS)]

        SMALL = 7 * 16

        def at(u, per, k=0):
            j, b = u
            return per * b + k if j is None else j * (2 * per) + (per * b + k)

        def prev(u):
            return (u[0], u[1] - 1)

        def nxt(u):
            return (u[0], u[1] + 1)

        def graph(u, g):
            j, b = u
            n = 2 * b + g
            return slice(n, n + 1) if j is None else bass.ds(j * 4 + n, 1)

        def first(u):
            return u[0] is None and u[1] == 0

        def tat(t, per, k=0):
            j, b = t
            return per * b + k if j is None else j * (NS * per) + (per * b + k)

        def round_of(t, per):
            j, b = t
            r = per * (b // NS + 1)
            return r if j is None else j * per + r

        def half_round(t, per):
            j, b = t
            r = per * (b // 2 + 1)
            return r if j is None else j * (NS // 2 * per) + r

        def early(eng, value):
            return value if isinstance(value, int) else eng.snap(eng.to_reg(value))

        def over(body, eng, lo, hi):
            with eng.Fori(0, (hi - lo) // 2) as j:
                body((j, lo))
                body((j, lo + 1))

        block = ctx.enter_context(nc.Block())

        x_g = x.rearrange("b (q p) d -> p b q d", p=P)
        adj_g = adj.rearrange("b (q p) m -> b p q m", p=P)
        out_g = out.rearrange("b (q p) d -> b p q d", p=P)
        res_g = result_rows.rearrange("(b q p k) d -> b p q (k d)", q=Q, p=P, k=K)

        @block.sync
        def _(sp):
            sp.dma_start(x_all[:, 0:2], x_g[:, 0:2]).then_inc(x0_loaded, 16)
            for g in range(2):
                sp.dma_start(adj_sb[g][:, :, :], adj_g[g]).then_inc(adj_loaded[g], 16)
            sp.dma_start(x_all[:, 2:B], x_g[:, 2:B]).then_inc(xrest_loaded, 16)

            def load_adj(u, g):
                sp.wait_ge(adj_turned, at(prev(u), UT, Q * g + Q))
                j, b = u
                src = adj_g[2 * b + g] if j is None else adj_g[bass.ds(j * 4 + (2 * b + g), 1)].rearrange("o p q m -> p (o q) m")
                sp.dma_start(adj_sb[g][:, :, :], src).then_inc(adj_loaded[g], 16)

            for g in range(2):
                load_adj((None, 1), g)
            sp.dma_start(wpack[:, :, 0:H], w1.rearrange("e d h -> d e h")).then_inc(weights_loaded, 16)
            for e in range(E):
                sp.dma_start(wpack[:, e, O_W2:O_B2].rearrange("p (c d) -> p c d", d=D),
                             w2[e].rearrange("(c p) d -> p c d", p=P)).then_inc(weights_loaded, 16)
            sp.dma_start(wpack[:, :, O_B2:O_B1], b2.partition_broadcast(P)).then_inc(weights_loaded, 16)
            sp.wait_ge(dve_const, 4)
            sp.dma_start(sorted_rows[DUMMY:DUMMY + TILE, :].rearrange("(p j) c -> p (j c)", j=2),
                         pad_tile[:, :, :].rearrange("p j c -> p (j c)")).then_inc(dummy_written, 16)

            def both(u):
                load_adj(u, 0)
                load_adj(u, 1)

            over(both, sp, 2, UNITS)

            sp.wait_ge(table, 20)
            for e in range(E):
                row = sp.value_load(tab_pad[0:1, e:e + 1], min_val=0, max_val=DUMMY - TILE)
                sp.dma_start(sorted_rows[bass.ds(row, TILE), :].rearrange("(p j) c -> p (j c)", j=2),
                             pad_tile[:, :, :].rearrange("p j c -> p (j c)")).then_inc(pads_written, 16)
            sp.wait_ge(wpack_ready, 1)
            sp.wait_ge(w1_scaled, E)

            def load_tile(t):
                j, b = t
                s = b % NS
                col = slice(b, b + 1) if j is None else bass.ds(j * NS + b, 1)
                off = sp.value_load(tab_e[0:1, col], min_val=0, max_val=(E - 1) * WP)
                row = sp.value_load(tab_row[0:1, col], min_val=0, max_val=DUMMY)
                sp.dma_start(wbuf[s][:, :], wpack[:, :, :].rearrange("p e w -> p (e w)")[:, bass.ds(off, WP)])\
                    .then_inc(wbuf_loaded[s], 16)
                sp.dma_start(xt[s][:, :, :].rearrange("p j c -> p (j c)"),
                             sorted_rows[bass.ds(row, TILE), :].rearrange("(p j) c -> p (j c)", j=2))\
                    .then_inc(xt_loaded[s], 16)

            for u in range(2):
                sp.wait_ge(scattered[u], UNITS // 2 * UT * K * 16)
            sp.wait_ge(dummy_written, 16)
            sp.wait_ge(pads_written, 16 * E)
            for b in range(NS):
                load_tile((None, b))
            with sp.Fori(0, TILES // NS - 1) as j:
                for b in range(NS):
                    used = early(sp, tat((j, b), 2, 2))
                    sent = early(sp, half_round((j, b), 32))
                    sp.wait_ge(ys_ready, used)
                    sp.wait_ge(y_scattered[b % 2], sent)
                    load_tile((j, b + NS))

            for s in range(2):
                sp.wait_ge(y_scattered[s], TILES // 2 * 32)
            for s in range(NS):
                sp.dma_start(y2[s], res_g[s]).then_inc(y2_loaded[s], 16)
            with sp.Fori(0, B // NS - 1) as j:
                for s in range(NS):
                    sp.wait_ge(sum2, j * NS + (s + 1))
                    sp.dma_start(y2[s], res_g[bass.ds(j * NS + (s + NS), 1)].rearrange("o p q c -> p (o q) c"))\
                        .then_inc(y2_loaded[s], 16)

        @block.scalar
        def _(act):
            act.dma_start(wg_sb[:, :], gnn_w).then_inc(small_loaded, 16)
            act.dma_start(bias_row[:, :, :], gnn_b.unsqueeze(0).unsqueeze(0).to_broadcast([1, Q, D])).then_inc(small_loaded, 16)
            act.dma_start(wr_sb[:, :], wr).then_inc(small_loaded, 16)
            act.dma_start(br_sb[:, :], br.partition_broadcast(P)).then_inc(small_loaded, 16)
            act.dma_start(vecs[0:E * HC, :], b1.rearrange("e (c p) -> (e c) p", p=P)).then_inc(small_loaded, 16)
            act.dma_start(vecs[E * HC:E * HC + E, :], ln_g).then_inc(small_loaded, 16)
            act.dma_start(vecs[E * HC + E:VR, :], ln_b).then_inc(small_loaded, 16)

            def norm_x(u, g):
                act.wait_ge(pool_const, 1)
                act.wait_ge(ln1, at(u, 14, 14))
                if not first(u):
                    act.wait_ge(pool_const, 1)
                    act.wait_ge(g_done, at(prev(u), 2, g + 1))
                for q in range(Q):
                    t = g * Q + q
                    act.activation(xn[g][:, q, :], x_all[:, graph(u, g), q, :].rearrange("p o d -> p (o d)"), ACT.Identity,
                                   bias=nmr1[:, t:t + 1], scale=rstd1[:, t:t + 1]).then_inc(xn_ready, 1)

            def copy_adjT(u, g):
                if not first(u):
                    act.wait_ge(g_done, at(prev(u), 2, g + 1))
                for r in range(Q):
                    act.wait_ge(adj_turned, at(u, UT, g * Q + r + 1))
                    act.activation(adjT[g][:, r, :], psT[r % 2][:, :], ACT.Copy).then_inc(adjT_ready, 1)

            def copy_gT(u, g):
                if not first(u):
                    act.wait_ge(w_done, at(prev(u), 2, g + 1))
                act.wait_ge(g_done, at(u, 2, g + 1))
                act.activation(gT[g][:, :], psG[:, :], ACT.Copy).then_inc(gT_ready, 1)

            def copy_zT(u, g):
                if not first(u):
                    act.wait_ge(l_done, at(prev(u), 2, g + 1))
                act.wait_ge(z_turned, at(u, 2, g + 1))
                act.activation(zT[g][:, :], psZ[g][:, :], ACT.Copy).then_inc(zT_ready, 1)

            def exp_gap(u):
                act.wait_ge(route, at(u, 23, 9))
                act.activation(e2[:, :], gap[:, :], ACT.Exp).then_inc(exp_ready, 1)

            def unit(u, last=False):
                copy_gT(u, 0)
                copy_adjT(u, 1)
                if not first(u):
                    copy_zT(prev(u), 0)
                    copy_zT(prev(u), 1)
                if not last:
                    norm_x(nxt(u), 0)
                copy_gT(u, 1)
                if not last:
                    norm_x(nxt(u), 1)
                    copy_adjT(nxt(u), 0)
                if not first(u):
                    exp_gap(prev(u))

            norm_x((None, 0), 0)
            norm_x((None, 0), 1)
            copy_adjT((None, 0), 0)
            unit((None, 0))
            act.wait_ge(b1_done, 1)
            for e in range(E):
                act.activation(wpack[:, e, 0:H], wpack[:, e, 0:H], ACT.Identity, scale=gcol[:, e:e + 1]).then_inc(w1_scaled, 1)
            unit((None, 1))
            over(unit, act, 2, UNITS - 2)
            unit((None, UNITS - 2))
            unit((None, UNITS - 1), last=True)
            copy_zT((None, UNITS - 1), 0)
            copy_zT((None, UNITS - 1), 1)
            exp_gap((None, UNITS - 1))

            def gelu(t, b1_slot, p):
                if t[0] is not None or t[1] >= 2:
                    act.wait_ge(pool_const, 1)
                    act.wait_ge(y_done, tat((t[0], t[1] - 1), 1))
                for c in range(HC):
                    act.wait_ge(h_done, tat(t, HC, c + 1))
                    act.activation(hT[p][:, c, :], psH[c][:, 0:TILE], ACT.Gelu,
                                   bias=wbuf[b1_slot][:, O_B1 + c:O_B1 + c + 1]).then_inc(gelu_done, 1)

            for b in range(NS):
                gelu((None, b), b, b % 2)
            with act.Fori(0, TILES // NS - 1) as j:
                for b in range(NS):
                    gelu((j, b + NS), b, b % 2)

            for s in range(NS):
                act.wait_ge(sum2, s + 1)
                act.dma_start(out_g[s], fin[s]).then_inc(stored[s], 16)
            with act.Fori(0, B // NS - 1) as j:
                for s in range(NS):
                    act.wait_ge(sum2, j * NS + (NS + s + 1))
                    act.dma_start(out_g[bass.ds(j * NS + (s + NS), 1)].rearrange("o p q d -> p (o q) d"), fin[s])\
                        .then_inc(stored[s], 16)
            for s in range(NS):
                act.wait_ge(stored[s], B // NS * 16)

        @block.tensor
        def _(pe):
            def turn_adj(u, g):
                pe.wait_ge(adj_loaded[g], at(u, 16, 16))
                for r in range(Q):
                    if not (first(u) and g == 0 and r < 2):
                        pe.wait_ge(adjT_ready, at(u, UT, g * Q + r - 1))
                    for q in range(Q):
                        last = nc.tensor.transpose(psT[r % 2][:, q * P:(q + 1) * P], adj_sb[g][:, q, r * P:(r + 1) * P], ident[:, :])
                    last.then_inc(adj_turned, 1)

            def aggregate(u, g):
                pe.wait_ge(xn_ready, at(u, UT, Q * (g + 1)))
                pe.wait_ge(adjT_ready, at(u, UT, Q * (g + 1)))
                if not (first(u) and g == 0):
                    pe.wait_ge(gT_ready, at(u, 2, g))
                for r in range(Q):
                    last = nc.tensor.matmul(psG[:, :], xn[g][:, r, :], adjT[g][:, r, :], start=(r == 0), stop=(r == Q - 1))
                last.then_inc(g_done, 1)

            def project(u, g):
                if not first(u):
                    pe.wait_ge(x1_ready, at(prev(u), 2, g + 1))
                nc.tensor.matmul(psO[g][:, :], ones_row[:, :], bias_row[:, :, :].rearrange("o q d -> o (q d)"), start=True, stop=False)
                pe.wait_ge(gT_ready, at(u, 2, g + 1))
                for q in range(Q):
                    last = nc.tensor.matmul(psO[g][:, q * D:(q + 1) * D], gT[g][:, q * P:(q + 1) * P], wg_sb[:, :],
                                            start=False, stop=(q == Q - 1))
                last.then_inc(w_done, 1)

            def turn_z(u, g):
                pe.wait_ge(ln2, at(u, 25, 16 + Q * (g + 1)))
                if not first(u):
                    pe.wait_ge(zT_ready, at(prev(u), 2, g + 1))
                for q in range(Q):
                    last = nc.tensor.transpose(psZ[g][:, q * P:(q + 1) * P], z[g][:, q, :], ident[:, :])
                last.then_inc(z_turned, 1)

            def logits(u, g):
                pe.wait_ge(zT_ready, at(u, 2, g + 1))
                if not first(u) and g == 0:
                    pe.wait_ge(route, at(prev(u), 23, 23))
                for q in range(Q):
                    last = nc.tensor.matmul(psL[:, g * Q + q, :], zT[g][:, q * P:(q + 1) * P], wr_sb[:, :], start=True, stop=True)
                last.then_inc(l_done, 1)

            def rank(u):
                pe.wait_ge(route, at(u, 23, 14))
                nc.tensor.matmul(psR[:, :, :], before[:, :], sel[:, :, :], start=True, stop=False)
                nc.tensor.matmul(psR[:, :, :], ones[:, :], sel_before[:, :].unsqueeze(1).to_broadcast([P, UT, E]), start=False, stop=False)
                for t in range(UT - 1):
                    last = nc.tensor.matmul(psR[:, t + 1:UT, :], ones[:, :],
                                            sel[:, t:t + 1, :].to_broadcast([P, UT - 1 - t, E]), start=False, stop=(t == UT - 2))
                last.then_inc(rank_done, 1)

            def unit(u, last=False):
                aggregate(u, 0)
                turn_adj(u, 1)
                project(u, 0)
                if not first(u):
                    turn_z(prev(u), 0)
                    turn_z(prev(u), 1)
                aggregate(u, 1)
                if not first(u):
                    logits(prev(u), 0)
                    logits(prev(u), 1)
                if not last:
                    turn_adj(nxt(u), 0)
                project(u, 1)
                if not first(u):
                    rank(prev(u))

            pe.wait_ge(pool_const, 6)
            pe.wait_ge(dve_const, 4)
            pe.wait_ge(small_loaded, SMALL)
            nc.tensor.transpose(psVec, vecs[:, :], ident[0:VR, 0:VR]).then_inc(vecs_turned, 1)
            turn_adj((None, 0), 0)
            unit((None, 0))
            pe.wait_ge(weights_loaded, (E + 2) * 16)
            pe.wait_ge(vecT_ready, 1)
            for e in range(E):
                for c in range(HC):
                    last = nc.tensor.matmul(psB1[:, e * HC + c:e * HC + c + 1], wpack[:, e, c * P:(c + 1) * P], bcol[:, e:e + 1],
                                            start=True, stop=True)
            last.then_inc(b1_done, 1)
            pe.wait_ge(wpack_ready, 1)
            unit((None, 1))
            over(unit, pe, 2, UNITS - 2)
            unit((None, UNITS - 2))
            unit((None, UNITS - 1), last=True)
            end = (None, UNITS - 1)
            for g in range(2):
                turn_z(end, g)
            for g in range(2):
                logits(end, g)
            rank(end)
            pe.wait_ge(route, at(end, 23, 23))
            nc.tensor.matmul(psCnt, ones[:, :], sel_before[:, :], start=True, stop=True).then_inc(counted, 1)

            def turn_x(t, s):
                pe.wait_ge(xt_loaded[s], round_of(t, 16))
                if t[0] is not None or t[1] >= 1:
                    pe.wait_ge(xT_ready, tat(t, 1))
                for h in range(2):
                    last = nc.tensor.transpose(psX[:, h * P:(h + 1) * P], xt[s][:, h, 0:D], ident[:, :])
                last.then_inc(xt_turned, 1)

            def up(t, s):
                pe.wait_ge(wbuf_loaded[s], round_of(t, 16))
                pe.wait_ge(xT_ready, tat(t, 1, 1))
                for c in range(HC):
                    if t[0] is not None or t[1] >= 1:
                        pe.wait_ge(gelu_done, tat((t[0], t[1] - 1), HC, c + 1))
                    nc.tensor.matmul(psH[c][:, 0:TILE], wbuf[s][:, c * P:(c + 1) * P], xT[s % 2][:, :], start=True, stop=True)\
                        .then_inc(h_done, 1)

            def down(t, s):
                pe.wait_ge(gelu_done, tat(t, HC, HC))
                if t[0] is not None or t[1] >= 2:
                    pe.wait_ge(yb_ready, tat((t[0], t[1] - 1), 1))
                for h in range(2):
                    for c in range(HC):
                        last = nc.tensor.matmul(psY[s % 2][:, h * D:(h + 1) * D], hT[s % 2][:, c, h * P:(h + 1) * P],
                                                wbuf[s][:, O_W2 + c * D:O_W2 + (c + 1) * D], start=(c == 0), stop=(c == HC - 1))
                last.then_inc(y_done, 1)

            pe.wait_ge(table, 2)
            turn_x((None, 0), 0)
            up((None, 0), 0)
            turn_x((None, 1), 1)
            def step(t, ups=True, turns=True):
                b = t[1]
                if ups:
                    up((t[0], b + 1), (b + 1) % NS)
                if turns:
                    turn_x((t[0], b + 2), (b + 2) % NS)
                down(t, b % NS)

            step((None, 0))
            step((None, 1))
            step((None, 2))
            step((None, 3))
            with pe.Fori(0, TILES // NS - 2) as j:
                for b in range(NS):
                    step((j, b + NS))
            for b in range(TILES - NS, TILES):
                step((None, b), ups=b + 1 < TILES, turns=b + 2 < TILES)

        @block.vector
        def _(dve):
            V = nc.vector
            V.memset(ones[:, :], 1.0).then_inc(dve_const, 1)
            V.memset(ones_row[:, :], 1.0).then_inc(dve_const, 1)
            V.memset(pad_tile[:, :, :], 0.0).then_inc(dve_const, 1)
            dve.wait_ge(dve_const, 3)
            V.memset(pad_tile[:, :, D:D + 1].bitcast(I32), int(NOWHERE)).then_inc(dve_const, 1)
            V.memset(sel_before[:, :], 0.0).then_inc(dve_const, 1)
            V.memset(one8[:, :], 1.0).then_inc(dve_const, 1)
            dve.wait_ge(pool_const, 6)
            V.tensor_scalar(region_of[:, :], iota_i[:, 0:E], float(REGION), None, ALU.mult).then_inc(dve_const, 1)
            V.tensor_scalar(prefer_low[:, :], iota_i[:, 0:E], -1.0, float(E), ALU.mult, ALU.add).then_inc(dve_const, 1)
            V.tensor_scalar(thr[:, :], iota_i[0:1, 0:MAXT], float(TILE), None, ALU.mult).then_inc(dve_const, 1)
            V.tensor_copy(tnum[:, :], iota_i[0:1, 0:TILES]).then_inc(dve_const, 1)
            V.tensor_scalar(tnum8[:, :], iota_i[0:1, 0:TILES], float(TILE), float(-DUMMY), ALU.mult, ALU.add).then_inc(dve_const, 1)
            dve.wait_ge(small_loaded, SMALL)
            dve.wait_ge(dve_const, 11)

            dve.wait_ge(vecs_turned, 1)
            V.tensor_copy(vecT[:, :], psVec).then_inc(vecT_ready, 1)

            def spread(st, d, v, s, q, var, chain, base):
                dve.wait_ge(chain, base(8))
                V.tensor_tensor(d[:, :], st[:, :, 1], st[:, :, 4], ALU.subtract).then_inc(chain, 1)
                V.tensor_tensor(v[:, :], st[:, :, 2], st[:, :, 5], ALU.add).then_inc(chain, 1)
                V.tensor_tensor(s[:, :], st[:, :, 1], st[:, :, 4], ALU.add).then_inc(chain, 1)
                dve.wait_ge(chain, base(9))
                V.scalar_tensor_tensor(q[:, :], d[:, :], 0.25, d[:, :], ALU.mult, ALU.mult).then_inc(chain, 1)
                dve.wait_ge(chain, base(12))
                V.scalar_tensor_tensor(var[:, :], v[:, :], 1.0 / D, q[:, :], ALU.mult, ALU.add).then_inc(chain, 1)

            def norm1(u):
                if first(u):
                    dve.wait_ge(x0_loaded, 16)
                else:
                    dve.wait_ge(xrest_loaded, 16)
                    dve.wait_ge(xn_ready, at(prev(u), UT, UT))
                for t in range(UT):
                    V.bn_stats(st1[:, t, :], x_all[:, graph(u, t // Q), t % Q, :].rearrange("p o d -> p (o d)")).then_inc(ln1, 1)
                spread(st1, d1, v1, s1, q1, var1, ln1, lambda k: at(u, 14, k))
                dve.wait_ge(rstd1_ready, at(u, 2, 2))
                V.scalar_tensor_tensor(nmr1[:, :], s1[:, :], -0.5, rstd1[:, :], ALU.mult, ALU.mult).then_inc(ln1, 1)

            def residual(u, g):
                dve.wait_ge(w_done, at(u, 2, g + 1))
                xs = x_all[:, graph(u, g), :, :].rearrange("p o q d -> p (o q d)")
                V.tensor_tensor(xs, psO[g][:, :], xs, ALU.add).then_inc(x1_ready, 1)

            def norm2(u):
                both_in = early(dve, at(u, 2, 2))
                dve.wait_ge(dve_const, 11)
                dve.wait_ge(x1_ready, both_in)
                for t in range(UT):
                    V.bn_stats(st2[:, t, :], x_all[:, graph(u, t // Q), t % Q, :].rearrange("p o d -> p (o d)")).then_inc(ln2, 1)
                spread(st2, d2, v2, s2, q2, var2, ln2, lambda k: at(u, 25, k))
                V.tensor_scalar(mean2[:, :], s2[:, :], 0.5, None, ALU.mult).then_inc(ln2, 1)
                dve.wait_ge(rstd2_ready, at(u, 2, 2))
                V.tensor_tensor(t2[:, :], var2[:, :], rstd2[:, :], ALU.mult).then_inc(ln2, 1)
                dve.wait_ge(ln2, at(u, 25, 15))
                V.tensor_tensor(u2[:, :], t2[:, :], rstd2[:, :], ALU.mult).then_inc(ln2, 1)
                if not first(u):
                    dve.wait_ge(z_turned, at(prev(u), 2, 2))
                for t in range(UT):
                    g, q = divmod(t, Q)
                    V.tensor_scalar(z[g][:, q, :], x_all[:, graph(u, g), q, :].rearrange("p o d -> p (o d)"),
                                    mean2[:, t:t + 1], rstd2[:, t:t + 1], ALU.subtract, ALU.mult).then_inc(ln2, 1)
                dve.wait_ge(rstd3_ready, at(u, 2, 2))
                V.tensor_tensor(scale3[:, :], rstd2[:, :], rstd3[:, :], ALU.mult).then_inc(ln2, 1)

            def make_rows(u, par, fresh):
                if not fresh:
                    j, b = u
                    n = UT * K * 16
                    dve.wait_ge(scattered[par], n * (b // 2) if j is None else j * n + n * (b // 2))
                dve.wait_ge(ln2, at(u, 25, 25))
                for t in range(UT):
                    V.tensor_scalar(rows[par][:, t, :, 0:D],
                                    x_all[:, graph(u, t // Q), t % Q, :].to_broadcast([P, K, D]),
                                    mean2[:, t:t + 1], scale3[:, t:t + 1], ALU.subtract, ALU.mult).then_inc(rows_ready, 1)
                idx = rows[par][:, :, :, D:D + 1].bitcast(I32)
                V.tensor_scalar(idx, idx, 4.0 * N * K, None, ALU.add).then_inc(rows_ready, 1)

            def choose(u, par):
                r = lambda k: at(u, 23, k)
                def e8(ap):
                    return ap[:, :].unsqueeze(2).to_broadcast([P, UT, E])
                dve.wait_ge(l_done, at(u, 2, 2))
                V.tensor_tensor(lg[:, :, :], psL[:, :, :], br_sb[:, :].unsqueeze(1).to_broadcast([P, UT, E]), ALU.add).then_inc(route, 1)
                dve.wait_ge(route, r(1))
                V.tensor_reduce(top1[:, :], lg[:, :, :], AX.X, ALU.max).then_inc(route, 1)
                dve.wait_ge(route, r(2))
                V.tensor_tensor(eq1[:, :, :], lg[:, :, :], e8(top1), ALU.is_equal).then_inc(route, 1)
                dve.wait_ge(route, r(3))
                V.tensor_tensor(kk1[:, :, :], eq1[:, :, :], prefer_low[:, :].unsqueeze(1).to_broadcast([P, UT, E]), ALU.mult).then_inc(route, 1)
                dve.wait_ge(route, r(4))
                V.tensor_reduce(key1[:, :], kk1[:, :, :], AX.X, ALU.max).then_inc(route, 1)
                dve.wait_ge(route, r(5))
                V.tensor_tensor(onehot[:, 0, :, :], kk1[:, :, :], e8(key1), ALU.is_equal).then_inc(route, 1)
                dve.wait_ge(route, r(6))
                V.scalar_tensor_tensor(lg2[:, :, :], onehot[:, 0, :, :], -BIG, lg[:, :, :], ALU.mult, ALU.add).then_inc(route, 1)
                dve.wait_ge(route, r(7))
                V.tensor_reduce(top2[:, :], lg2[:, :, :], AX.X, ALU.max).then_inc(route, 1)
                dve.wait_ge(route, r(8))
                V.tensor_tensor(gap[:, :], top2[:, :], top1[:, :], ALU.subtract).then_inc(route, 1)
                V.tensor_tensor(eq2[:, :, :], lg2[:, :, :], e8(top2), ALU.is_equal).then_inc(route, 1)
                dve.wait_ge(route, r(10))
                V.tensor_tensor(kk2[:, :, :], eq2[:, :, :], prefer_low[:, :].unsqueeze(1).to_broadcast([P, UT, E]), ALU.mult).then_inc(route, 1)
                dve.wait_ge(route, r(11))
                V.tensor_reduce(key2[:, :], kk2[:, :, :], AX.X, ALU.max).then_inc(route, 1)
                dve.wait_ge(route, r(12))
                V.tensor_tensor(onehot[:, 1, :, :], kk2[:, :, :], e8(key2), ALU.is_equal).then_inc(route, 1)
                dve.wait_ge(route, r(13))
                V.tensor_tensor(sel[:, :, :], onehot[:, 0, :, :], onehot[:, 1, :, :], ALU.add).then_inc(route, 1)
                dve.wait_ge(exp_ready, at(u, 1, 1))
                V.tensor_scalar(den[:, :], e2[:, :], 1.0, None, ALU.add).then_inc(route, 1)
                dve.wait_ge(route, r(15))
                V.reciprocal(rows[par][:, :, 0, D + 1], den[:, :]).then_inc(route, 1)
                dve.wait_ge(route, r(16))
                V.tensor_tensor(rows[par][:, :, 1, D + 1], rows[par][:, :, 0, D + 1], e2[:, :], ALU.mult).then_inc(route, 1)
                dve.wait_ge(rank_done, at(u, 1, 1))
                V.tensor_tensor(pos[:, :, :], psR[:, :, :], region_of[:, :].unsqueeze(1).to_broadcast([P, UT, E]), ALU.add).then_inc(route, 1)
                dve.wait_ge(route, r(18))
                for k in range(K):
                    V.tensor_tensor(place[:, k, :, :], onehot[:, k, :, :], pos[:, :, :], ALU.mult).then_inc(route, 1)
                dve.wait_ge(route, r(20))
                with nc.allow_low_precision(reason="a sum of one whole number below 2^24 and zeros"):
                    V.tensor_reduce(slot[par][:, :, :], place[:, :, :, :], AX.X, ALU.add).then_inc(route, 1)
                V.tensor_reduce(sel_sum[:, :], sel[:, :, :].rearrange("p t e -> p e t"), AX.X, ALU.add).then_inc(route, 1)
                dve.wait_ge(route, r(22))
                V.tensor_tensor(sel_before[:, :], sel_before[:, :], sel_sum[:, :], ALU.add).then_inc(route, 1)

            def unit(u, last=False, fresh=False):
                if not first(u):
                    residual(prev(u), 1)
                    norm2(prev(u))
                if not last:
                    norm1(nxt(u))
                residual(u, 0)
                if not first(u):
                    par = (u[1] - 1) % 2
                    make_rows(prev(u), par, fresh)
                    choose(prev(u), par)

            norm1((None, 0))
            unit((None, 0))
            dve.wait_ge(b1_done, 1)
            V.tensor_tensor(wpack[:, :, O_B1:WP], psB1.rearrange("p (e c) -> p e c", c=HC),
                            vecT[:, 0:E * HC].rearrange("p (e c) -> p e c", c=HC), ALU.add)\
                .then_inc(wpack_ready, 1)
            unit((None, 1), fresh=True)
            unit((None, 2), fresh=True)
            over(unit, dve, 3, UNITS - 1)
            unit((None, UNITS - 1), last=True)
            end = (None, UNITS - 1)
            residual(end, 1)
            norm2(end)
            make_rows(end, end[1] % 2, False)
            choose(end, end[1] % 2)

            n = [0]

            def step(ins):
                n[0] += 1
                ins.then_inc(table, 1)
                dve.wait_ge(table, n[0])

            te = [1, TILES, E]
            dve.wait_ge(counted, 1)
            step(V.tensor_copy(cnt[:, :], psCnt[0:1, :]))
            step(V.tensor_tensor(base_row[:, :], cnt[:, :], region_of[0:1, :], ALU.add))
            step(V.tensor_copy(tab_pad[:, :], base_row[:, :]))
            step(V.tensor_tensor(more[:, :, :], cnt[:, :].unsqueeze(2).to_broadcast([1, E, MAXT]),
                                 thr[:, :].unsqueeze(1).to_broadcast([1, E, MAXT]), ALU.is_gt))
            step(V.tensor_reduce(nt[:, :], more[:, :, :], AX.X, ALU.add))
            step(V.tensor_tensor_scan(t_end[:, :], one8[:, :], nt[:, :], 0.0, ALU.mult, ALU.add))
            step(V.tensor_tensor(t_start[:, :], t_end[:, :], nt[:, :], ALU.subtract))
            step(V.tensor_tensor(ge_end[:, :, :], tnum[:, :].unsqueeze(2).to_broadcast(te), t_end[:, :].unsqueeze(1).to_broadcast(te), ALU.is_ge))
            step(V.tensor_tensor(ge_start[:, :, :], tnum[:, :].unsqueeze(2).to_broadcast(te), t_start[:, :].unsqueeze(1).to_broadcast(te), ALU.is_ge))
            step(V.tensor_tensor(mine[:, :, :], ge_start[:, :, :], ge_end[:, :, :], ALU.subtract))
            step(V.tensor_reduce(eid[:, :], ge_end[:, :, :], AX.X, ALU.add))
            step(V.tensor_scalar(tab_e[:, :], eid[:, :], float(E - 1), float(WP), ALU.min, ALU.mult))
            step(V.tensor_reduce(real[:, :], mine[:, :, :], AX.X, ALU.add))
            step(V.scalar_tensor_tensor(base_row[:, :], t_start[:, :], float(-TILE), region_of[0:1, :], ALU.mult, ALU.add))
            step(V.tensor_tensor(mine_row[:, :, :], mine[:, :, :], base_row[:, :].unsqueeze(1).to_broadcast(te), ALU.mult))
            step(V.tensor_reduce(row_a[:, :], mine_row[:, :, :], AX.X, ALU.add))
            step(V.tensor_tensor(row_b[:, :], real[:, :], tnum8[:, :], ALU.mult))
            step(V.tensor_tensor(row_a[:, :], row_a[:, :], row_b[:, :], ALU.add))
            step(V.tensor_scalar(row_b[:, :], row_a[:, :], float(DUMMY), None, ALU.add))
            step(V.tensor_copy(tab_row[:, :], row_b[:, :]))

            def copy_xT(t, s):
                if t[0] is not None or t[1] >= 2:
                    dve.wait_ge(h_done, tat((t[0], t[1] - 1), HC))
                dve.wait_ge(xt_turned, tat(t, 1, 1))
                V.tensor_copy(xT[s % 2][:, :], psX[:, 0:TILE]).then_inc(xT_ready, 1)

            def finish(t, s):
                dve.wait_ge(y_done, tat(t, 1, 1))
                V.tensor_tensor(yb[s % 2][:, :, :], psY[s % 2][:, 0:2 * D].rearrange("p (h d) -> p h d", h=2),
                                wbuf[s][:, O_B2:O_B1].unsqueeze(1).to_broadcast([P, 2, D]), ALU.add).then_inc(yb_ready, 1)
                if t[0] is not None or t[1] >= 2:
                    dve.wait_ge(y_scattered[s % 2], half_round((t[0], t[1] - 2), 32))
                dve.wait_ge(yb_ready, tat(t, 1, 1))
                for h in range(2):
                    V.tensor_scalar(ys[s % 2][:, h, :], yb[s % 2][:, h, :], xt[s][:, h, D + 1:D + 2], None, ALU.mult).then_inc(ys_ready, 1)

            copy_xT((None, 0), 0)
            copy_xT((None, 1), 1)

            def tile(t, copies=True):
                if copies:
                    copy_xT((t[0], t[1] + 2), (t[1] + 2) % NS)
                finish(t, t[1] % NS)

            for b in range(NS):
                tile((None, b))
            with dve.Fori(0, TILES // NS - 2) as j:
                for b in range(NS):
                    tile((j, b + NS))
            for b in range(TILES - NS, TILES):
                tile((None, b), copies=b + 2 < TILES)

            def combine(j, s, per0):
                gr = slice(s + per0, s + per0 + 1) if j is None else bass.ds(j * NS + (s + per0), 1)
                dve.wait_ge(y2_loaded[s], 16 if j is None else j * 16 + 32)
                xs = x_all[:, gr, :, :].rearrange("p o q d -> p (o q) d")
                V.tensor_tensor(xs, xs, y2[s][:, :, 0:D], ALU.add).then_inc(sum1, 1)
                if j is not None:
                    dve.wait_ge(stored[s], j * 16 + 16)
                dve.wait_ge(sum1, s + 1 if j is None else j * NS + (NS + s + 1))
                V.tensor_tensor(fin[s], xs, y2[s][:, :, D:2 * D], ALU.add).then_inc(sum2, 1)

            for s in range(NS):
                combine(None, s, 0)
            with dve.Fori(0, B // NS - 1) as j:
                for s in range(NS):
                    combine(j, s, NS)

        @block.gpsimd
        def _(pool):
            G = nc.gpsimd
            G.memset(ident[:, :], 0.0).then_inc(pool_const, 1)
            G.memset(before[:, :], 0.0).then_inc(pool_const, 1)
            G.memset(minus_half[:, :], -0.5).then_inc(pool_const, 1)
            pool.wait_ge(pool_const, 3)
            G.affine_select(out=ident[:, :], in_=ident[:, :], compare_op=ALU.not_equal, fill=1.0, base=0,
                            pattern=[[-1, P]], channel_multiplier=1).then_inc(pool_const, 1)
            G.affine_select(out=before[:, :], in_=before[:, :], compare_op=ALU.is_ge, fill=1.0, base=0,
                            pattern=[[-1, P]], channel_multiplier=1).then_inc(pool_const, 1)
            G.iota(iota_i[:, :], pattern=[[1, 80]], base=0, channel_multiplier=0).then_inc(pool_const, 1)
            for u in range(2):
                idx = rows[u][:, :, :, D:D + 1].bitcast(I32).rearrange("p t k o -> p t (k o)")
                G.iota(idx, pattern=[[K * P, UT], [1, K]], base=K * 2 * N * (u - 2), channel_multiplier=K).then_inc(pool_const, 1)

            def inv_sqrt(dst, src, ready, n):
                G.tensor_scalar(veps[:, :], src[:, :], LN_EPS, None, ALU.add).then_inc(ready, 1)
                pool.wait_ge(ready, n + 1)
                G.tensor_tensor(dst[:, :], veps[:, :], minus_half[:, :], ALU.pow).then_inc(ready, 1)

            def rstd_1(u):
                var1_in = early(pool, at(u, 14, 13))
                pool.wait_ge(pool_const, 8)
                pool.wait_ge(ln1, var1_in)
                inv_sqrt(rstd1, var1, rstd1_ready, at(u, 2))

            def rstd_23(u):
                var2_in = early(pool, at(u, 25, 13))
                u2_in = early(pool, at(u, 25, 16))
                pool.wait_ge(pool_const, 8)
                pool.wait_ge(ln2, var2_in)
                inv_sqrt(rstd2, var2, rstd2_ready, at(u, 2))
                pool.wait_ge(pool_const, 8)
                pool.wait_ge(ln2, u2_in)
                inv_sqrt(rstd3, u2, rstd3_ready, at(u, 2))

            def scatter(u, par, lo, hi):
                slots_in = early(pool, at(u, 23, 21))
                pool.wait_ge(pool_const, 8)
                pool.wait_ge(route, slots_in)
                for n in range(lo, hi):
                    t, k = divmod(n, K)
                    G.indirect_dma_start(out=sorted_rows, out_offset=bass.IndirectOffsetOnAxis(ap=slot[par][:, k, t:t + 1], axis=0),
                                         in_=rows[par][:, t, k, :], in_offset=None,
                                         bounds_check=DUMMY - 1, oob_is_err=False).then_inc(scattered[par], 16)

            NP = UT * K

            def unit(u, last=False):
                par = u[1] % 2
                scatter((u[0], u[1] - 2), par, 0, 2)
                rstd_23(prev(u))
                scatter((u[0], u[1] - 2), par, 2, NP // 2)
                if not last:
                    rstd_1(nxt(u))
                scatter((u[0], u[1] - 2), par, NP // 2, NP)

            rstd_1((None, 0))
            rstd_1((None, 1))
            rstd_23((None, 0))
            rstd_1((None, 2))
            over(unit, pool, 2, UNITS - 2)
            unit((None, UNITS - 2))
            unit((None, UNITS - 1), last=True)
            end = (None, UNITS - 1)
            scatter(prev(end), prev(end)[1] % 2, 0, 2)
            rstd_23(end)
            scatter(prev(end), prev(end)[1] % 2, 2, NP)
            scatter(end, end[1] % 2, 0, NP)

            def send(t, s):
                both_in = early(pool, tat(t, 2, 2))
                pool.wait_ge(pool_const, 8)
                pool.wait_ge(ys_ready, both_in)
                for h in range(2):
                    G.indirect_dma_start(out=result_rows,
                                         out_offset=bass.IndirectOffsetOnAxis(ap=xt[s][:, h, D:D + 1].bitcast(I32), axis=0),
                                         in_=ys[s % 2][:, h, :], in_offset=None,
                                         bounds_check=TOK * K - 1, oob_is_err=False).then_inc(y_scattered[s % 2], 16)

            with pool.Fori(0, TILES // NS) as j:
                for b in range(NS):
                    send((j, b), b)


_INS = ['x', 'adj', 'L0_gnn_weight', 'L0_gnn_bias', 'L0_ffn_Wr', 'L0_ffn_br', 'L0_ffn_ln_g', 'L0_ffn_ln_b',
        'L0_ffn_W1', 'L0_ffn_b1', 'L0_ffn_W2', 'L0_ffn_b2']


def kernel(**inputs):
    import numpy as _np
    import concourse.bacc as _bacc
    from concourse import mybir as _mybir
    from concourse.bass_utils import run_bass_kernel_spmd as _run

    nc = _bacc.Bacc("TRN2", target_bir_lowering=False, num_devices=1)
    arrays, args = {}, []
    for name in _INS:
        a = _np.ascontiguousarray(inputs[name])
        arrays[f"in_{name}_dram"] = a
        args.append(nc.dram_tensor(f"in_{name}_dram", a.shape, _mybir.dt.from_np(a.dtype), kind="ExternalInput").ap())
    out = nc.dram_tensor("out_dram", arrays["in_x_dram"].shape, _mybir.dt.float32, kind="ExternalOutput").ap()
    build(nc, *args, out)
    r = _run(nc, [arrays], core_ids=[0])
    return r.results[0]["out_dram"]
```

```python
import concourse.bass as bass
from concourse import mybir
from contextlib import ExitStack

FP32 = mybir.dt.float32
FP32R = mybir.dt.float32r
BF16 = mybir.dt.bfloat16
I32 = mybir.dt.int32
ALU = mybir.AluOpType
ACT = mybir.ActivationFunctionType
AX = mybir.AxisListType

P = 128
LN_EPS = 1e-5
BIG = 3.0e38


def build(nc, x, adj, gnn_w, gnn_b, wr, br, ln_g, ln_b, w1, b1, w2, b2, out):
    B, N, D = x.shape
    E = wr.shape[1]
    H = w1.shape[2]
    Q = N // P
    HC = H // P
    K = 2
    TOK = B * N
    UNITS = B // 2
    UT = 2 * Q
    J = 4
    TILE = J * P
    TILES = (TOK * K - E) // TILE + E
    REGION = TOK + TILE
    DUMMY = E * REGION
    RW = D + 2
    NOWHERE = 4 * TOK
    BW = HC + 1
    NS = 4
    MAXT = TOK // TILE
    MAGIC = 0x5F3759DF

    ctx = ExitStack()
    with ctx:
        def sb(name, shape, dt=FP32, stack=ctx):
            return stack.enter_context(nc.sbuf_tensor(name, shape, dt))

        def sem(name):
            return ctx.enter_context(nc.semaphore(name))

        sorted_rows = nc.dram_tensor("sorted_rows", [DUMMY + TILE, RW], FP32, kind="Internal").ap()
        result_rows = nc.dram_tensor("result_rows", [TOK * K, D], FP32, kind="Internal").ap()

        ident = sb("ident", [P, P])
        before = sb("before", [P, P], BF16)
        ones = sb("ones", [P, P], BF16)
        ones_row = sb("ones_row", [1, P])
        prefer_low = sb("prefer_low", [P, E])
        region_of = sb("region_of", [P, E])
        iota_i = sb("iota_i", [P, 64], I32)
        bias_row = sb("bias_row", [1, Q, D])
        wg_sb = sb("wg_sb", [P, D])
        wr_sb = sb("wr_sb", [P, E])
        br_sb = sb("br_sb", [P, E])
        VR = E * HC + 3 * E
        vecs = sb("vecs", [VR, P])
        vecT = sb("vecT", [P, VR])
        gcol = vecT[:, E * HC:E * HC + E]
        bcol = vecT[:, E * HC + E:E * HC + 2 * E]
        b2col = vecT[:, E * HC + 2 * E:VR]
        pad_tile = sb("pad_tile", [P, J, RW])

        x_all = sb("x_all", [P, B, Q, D])
        w1pack = sb("w1pack", [P, E, 2, H], FP32R)
        w2pack = sb("w2pack", [P, E, 2, HC * D], FP32R)
        bpack = sb("bpack", [P, E, BW])
        tab_e = sb("tab_e", [1, TILES], I32)
        tab_row = sb("tab_row", [1, TILES], I32)
        tab_pad = sb("tab_pad", [1, E], I32)

        part_a = ExitStack()
        def sa(name, shape, dt=FP32):
            return sb(name, shape, dt, part_a)
        adj_sb = [sa(f"adj_sb{g}", [P, Q, N]) for g in range(2)]
        adjT = [sa(f"adjT{g}", [P, Q, N]) for g in range(2)]
        xn = [sa(f"xn{g}", [P, Q, D]) for g in range(2)]
        gT = [sa(f"gT{g}", [P, N]) for g in range(2)]
        z = [sa(f"z{g}", [P, Q, D]) for g in range(2)]
        zT = [sa(f"zT{g}", [P, N]) for g in range(2)]
        w1raw = [sa(f"w1raw{s}", [P, H]) for s in range(2)]
        w2raw = [sa(f"w2raw{s}", [P, HC, D]) for s in range(2)]
        w1g = sa("w1g", [P, H])
        stats = sa("stats", [P, 2, UT, 6])
        dif, spr, tot, sq, var = (sa(n, [P, 2, UT]) for n in ("dif", "spr", "tot", "sq", "var"))
        arg = sa("arg", [P, 3, UT])
        half_bits = sa("half_bits", [P, 3, UT], I32)
        guess = sa("guess", [P, 3, UT])
        newton_a = sa("newton_a", [P, 3, UT])
        newton_b = sa("newton_b", [P, 3, UT])
        rstd = [sa(f"rstd{u}", [P, 3, UT]) for u in range(2)]
        mean2 = [sa(f"mean2_{u}", [P, UT]) for u in range(2)]
        shift = [sa(f"shift{u}", [P, 2, UT]) for u in range(2)]
        rows = [sa(f"rows{u}", [P, UT, K, RW]) for u in range(2)]
        slot = [sa(f"slot{u}", [P, K, UT], I32) for u in range(2)]
        lg = sa("lg", [P, UT, E])
        lg2 = sa("lg2", [P, UT, E])
        top1, top2, gap, key1, key2, e2, den = (
            sa(n, [P, UT]) for n in ("top1", "top2", "gap", "key1", "key2", "e2", "den"))
        eq1, eq2, kk1, kk2, pos = (sa(n, [P, UT, E]) for n in ("eq1", "eq2", "kk1", "kk2", "pos"))
        onehot = sa("onehot", [P, K, UT, E])
        sel = sa("sel", [P, UT, E], BF16)
        place = sa("place", [P, K, UT, E])
        sel_sum = sa("sel_sum", [P, E])
        sel_before = sa("sel_before", [P, E], BF16)
        cnt, nt, one8, t_end, t_start, base_row = (
            sa(n, [1, E]) for n in ("cnt", "nt", "one8", "t_end", "t_start", "base_row"))
        thr = sa("thr", [1, MAXT])
        more = sa("more", [1, E, MAXT])
        tnum, tnum8, eid, real, row_a, row_b = (
            sa(n, [1, TILES]) for n in ("tnum", "tnum8", "eid", "real", "row_a", "row_b"))
        ge_end, ge_start, mine, mine_row = (
            sa(n, [1, TILES, E]) for n in ("ge_end", "ge_start", "mine", "mine_row"))
        part_a.close()

        w1buf = [sb(f"w1buf{s}", [P, 2, H], FP32R) for s in range(2)]
        w2buf = [sb(f"w2buf{s}", [P, 2, HC * D], FP32R) for s in range(2)]
        bbuf = [sb(f"bbuf{s}", [P, BW]) for s in range(NS)]
        xt = [sb(f"xt{s}", [P, J, RW]) for s in range(NS)]
        x_hi = [sb(f"x_hi{s}", [P, TILE], FP32R) for s in range(2)]
        x_lo = [sb(f"x_lo{s}", [P, TILE], FP32R) for s in range(2)]
        h = sb("h", [P, HC, TILE])
        h_hi = [sb(f"h_hi{s}", [P, HC, TILE], FP32R) for s in range(2)]
        h_lo = [sb(f"h_lo{s}", [P, HC, TILE], FP32R) for s in range(2)]
        yT = sb("yT", [P, TILE])
        ys = [sb(f"ys{s}", [P, J, D]) for s in range(2)]
        result_row = [sb(f"result_row{s}", [P, J], I32) for s in range(2)]
        y2 = [sb(f"y2_{s}", [P, Q, K * D]) for s in range(NS)]
        fin = [sb(f"fin{s}", [P, Q, D]) for s in range(2)]

        bank = [ctx.enter_context(nc.psum_tensor(f"bank{i}", [P, 512], FP32)) for i in range(8)]
        psT = [bank[0], bank[1]]
        psG = bank[2]
        psO = [bank[3], bank[4]]
        psZ = [bank[5], psG]
        psL = bank[6][:, 0:UT * E].rearrange("p (t e) -> p t e", e=E)
        psB1 = bank[6][:, UT * E:UT * E + HC]
        psR = bank[7][:, 0:UT * E].rearrange("p (t e) -> p t e", e=E)
        psCnt = bank[7][:, UT * E:UT * E + E]
        psVec = bank[6][:, 384:384 + VR]
        psH = [bank[c] for c in range(HC)]
        psX = bank[4]
        psY = bank[5]
        psYt = bank[6]

        x_in = [sem(f"x_in{s}") for s in range(2)]
        small_loaded = sem("small_loaded")
        adj_loaded = [sem(f"adj_loaded{g}") for g in range(2)]
        raw_in = [sem(f"raw_in{s}") for s in range(2)]
        pool_const = sem("pool_const")
        dve_const = sem("dve_const")
        vecs_turned = sem("vecs_turned")
        vecT_ready = sem("vecT_ready")
        dummy_written = sem("dummy_written")
        stats_x = sem("stats_x")
        stats_x1 = sem("stats_x1")
        norm = sem("norm")
        z_ready = sem("z_ready")
        xn_ready = sem("xn_ready")
        adj_turned = sem("adj_turned")
        adjT_ready = sem("adjT_ready")
        g_done = sem("g_done")
        gT_ready = sem("gT_ready")
        w_done = sem("w_done")
        x1_ready = sem("x1_ready")
        z_turned = sem("z_turned")
        zT_ready = sem("zT_ready")
        l_done = sem("l_done")
        rows_ready = sem("rows_ready")
        route = sem("route")
        exp_ready = sem("exp_ready")
        rank_done = sem("rank_done")
        w_hi = sem("w_hi")
        w_lo = sem("w_lo")
        scattered = [sem(f"scattered{u}") for u in range(2)]
        rows_free = sem("rows_free")
        counted = sem("counted")
        table = sem("table")
        pads_written = sem("pads_written")
        w1_in = [sem(f"w1_in{s}") for s in range(2)]
        w2_in = [sem(f"w2_in{s}") for s in range(2)]
        xt_in = [sem(f"xt_in{s}") for s in range(NS)]
        xt_turned = sem("xt_turned")
        x_split = sem("x_split")
        h_done = sem("h_done")
        gelu_done = sem("gelu_done")
        hi_done = sem("hi_done")
        h_split = sem("h_split")
        y_done = sem("y_done")
        yT_ready = sem("yT_ready")
        y_turned = sem("y_turned")
        ys_ready = sem("ys_ready")
        y_scattered = [sem(f"y_scattered{s}") for s in range(2)]
        y2_loaded = [sem(f"y2_loaded{s}") for s in range(NS)]
        sum1 = sem("sum1")
        sum2 = sem("sum2")
        stored = [sem(f"stored{s}") for s in range(2)]

        SMALL = 8 * 16
        NORM = 20
        ROUTE = 24
        POOL_CONST = 7
        DVE_CONST = 12

        def at(u, per, k=0, step=2):
            j, b = u
            return per * b + k if j is None else j * (step * per) + (per * b + k)

        def tat(t, per, k=0):
            return at(t, per, k, NS)

        def by_slot(t, per, slots):
            j, b = t
            r = per * (b // slots + 1)
            return r if j is None else j * (NS // slots * per) + r

        def unit_slot(u, per):
            j, b = u
            r = per * (b // 2 + 1)
            return r if j is None else j * per + r

        def off(u, d):
            return (u[0], u[1] + d)

        def number(u, step, scale=1, add=0):
            j, b = u
            n = scale * b + add
            return n if j is None else j * (step * scale) + n

        def cut(n, size=1):
            return slice(n, n + size) if isinstance(n, int) else bass.ds(n, size)

        def graph(u, g):
            return cut(number(u, 2, 2, g))

        def real_unit(u):
            return u[0] is not None or 0 <= u[1] < UNITS

        def first(u):
            return u[0] is None and u[1] == 0

        def early(eng, value):
            return value if isinstance(value, int) else eng.snap(eng.to_reg(value))

        def walk(eng, body, lo, hi, loop_lo, loop_hi):
            for b in range(lo, loop_lo):
                body((None, b))
            with eng.Fori(0, (loop_hi - loop_lo) // 2) as j:
                body((j, loop_lo))
                body((j, loop_lo + 1))
            for b in range(loop_hi, hi):
                body((None, b))

        HEAD = NS
        TURNS = (TILES - 2 * NS + 1) // NS

        def walk_tiles(eng, body):
            for b in range(HEAD):
                body((None, b))
            with eng.Fori(0, TURNS) as j:
                for b in range(NS):
                    body((j, HEAD + b))
            for b in range(HEAD + NS * TURNS, TILES):
                body((None, b))

        def real_tile(t):
            return t[0] is not None or 0 <= t[1] < TILES

        block = ctx.enter_context(nc.Block())

        x_g = x.rearrange("b (q p) d -> p b q d", p=P)
        adj_g = adj.rearrange("b (q p) m -> b p q m", p=P)
        out_g = out.rearrange("b (q p) d -> b p q d", p=P)
        res_g = result_rows.rearrange("(b q p k) d -> b p q (k d)", q=Q, p=P, k=K)

        @block.sync
        def _(sp):
            def load_x(u):
                j, b = u
                if j is None:
                    src = x_g[:, 2 * b:2 * b + 2]
                else:
                    src = x_g[:, bass.ds(number(u, 2, 2), 2)]
                sp.dma_start(x_all[:, cut(number(u, 2, 2), 2)], src).then_inc(x_in[b % 2], 16)

            def load_adj(u, g):
                if not first(u):
                    sp.wait_ge(adj_turned, at(off(u, -1), UT, Q * g + Q))
                sp.dma_start(adj_sb[g][:, :, :], adj_g[cut(number(u, 2, 2, g))].rearrange("o p q m -> p (o q) m"))\
                    .then_inc(adj_loaded[g], 16)

            def load_raw(u):
                s = u[1] % 2
                if u[0] is not None or u[1] >= 2:
                    used_b1 = early(sp, at(off(u, -2), 2, 2))
                    sp.wait_ge(w_lo, at(off(u, -2), 2, 2))
                    sp.wait_ge(l_done, used_b1)
                e = cut(number(u, 2))
                sp.dma_start(w1raw[s][:, :], w1[e].rearrange("o d h -> d (o h)")).then_inc(raw_in[s], 16)
                sp.dma_start(w2raw[s][:, :, :], w2[e].rearrange("o (c p) d -> p (o c) d", p=P)).then_inc(raw_in[s], 16)

            load_x((None, 0))
            for g in range(2):
                load_adj((None, 0), g)
            load_x((None, 1))
            load_raw((None, 0))
            load_raw((None, 1))
            sp.wait_ge(dve_const, 4)
            sp.dma_start(sorted_rows[DUMMY:DUMMY + TILE, :].rearrange("(p j) c -> p (j c)", j=J),
                         pad_tile[:, :, :].rearrange("p j c -> p (j c)")).then_inc(dummy_written, 16)

            def unit(u):
                if real_unit(off(u, 1)):
                    load_adj(off(u, 1), 0)
                if u[0] is not None or u[1] + 2 < UNITS:
                    sp.wait_ge(norm, at(u, NORM, 1))
                    load_x(off(u, 2))
                if real_unit(off(u, 1)):
                    load_adj(off(u, 1), 1)
                if not first(u) and real_unit(off(u, 1)):
                    load_raw(off(u, 1))

            walk(sp, unit, 0, UNITS, 1, UNITS - 3)

            sp.wait_ge(table, 20)
            for e in range(E):
                row = sp.value_load(tab_pad[0:1, e:e + 1], min_val=0, max_val=DUMMY - TILE)
                sp.dma_start(sorted_rows[bass.ds(row, TILE), :].rearrange("(p j) c -> p (j c)", j=J),
                             pad_tile[:, :, :].rearrange("p j c -> p (j c)")).then_inc(pads_written, 16)

            def expert_of(t):
                return sp.value_load(tab_e[0:1, cut(number(t, NS))], min_val=0, max_val=E - 1)

            def row_of(t):
                return sp.value_load(tab_row[0:1, cut(number(t, NS))], min_val=0, max_val=DUMMY)

            def load_w(t, e, pack, buf, sems):
                s = t[1] % 2
                sp.dma_start(buf[s][:, :, :].rearrange("p a n -> p (a n)").bitcast(FP32),
                             pack[:, cut(e), :, :].rearrange("p o a n -> p (o a n)").bitcast(FP32)).then_inc(sems[s], 16)

            def load_rows(t, e, row):
                s = t[1] % NS
                sp.dma_start(xt[s][:, :, :].rearrange("p j c -> p (j c)"),
                             sorted_rows[bass.ds(row, TILE), :].rearrange("(p j) c -> p (j c)", j=J)).then_inc(xt_in[s], 16)
                sp.dma_start(bbuf[s][:, :], bpack[:, cut(e), :].rearrange("p o b -> p (o b)")).then_inc(xt_in[s], 16)

            sp.wait_ge(w_lo, 2 * UNITS)
            sp.wait_ge(rows_ready, 9 * UNITS)
            for b in range(2):
                e = expert_of((None, b))
                load_w((None, b), e, w1pack, w1buf, w1_in)
                load_w((None, b), e, w2pack, w2buf, w2_in)
            for u in range(2):
                sp.wait_ge(scattered[u], UNITS // 2 * UT * K * 16)
            sp.wait_ge(dummy_written, 16)
            sp.wait_ge(pads_written, 16 * E)
            for b in range(3):
                load_rows((None, b), expert_of((None, b)), row_of((None, b)))
            e = expert_of((None, 2))
            sp.wait_ge(h_done, HC)
            load_w((None, 2), e, w1pack, w1buf, w1_in)

            def tile(t):
                if real_tile(off(t, 3)):
                    e3rd, row = expert_of(off(t, 3)), row_of(off(t, 3))
                    sp.wait_ge(h_done, tat(t, HC, 2 * HC))
                    load_w(off(t, 3), e3rd, w1pack, w1buf, w1_in)
                    if t[0] is not None or t[1] >= 1:
                        sp.wait_ge(ys_ready, tat(off(t, -1), 2, 2))
                    load_rows(off(t, 3), e3rd, row)
                if real_tile(off(t, 2)):
                    e2nd = expert_of(off(t, 2))
                    used_w2 = early(sp, tat(t, 1, 1))
                    sp.wait_ge(table, 20)
                    sp.wait_ge(y_done, used_w2)
                    load_w(off(t, 2), e2nd, w2pack, w2buf, w2_in)

            walk_tiles(sp, tile)

            for s in range(2):
                sp.wait_ge(y_scattered[s], (TILES + 1 - s) // 2 * J * 16)
            for s in range(NS):
                sp.dma_start(y2[s][:, :, :], res_g[s]).then_inc(y2_loaded[s], 16)
            with sp.Fori(0, B // NS - 1) as j:
                for s in range(NS):
                    sp.wait_ge(sum2, j * NS + (s + 1))
                    sp.dma_start(y2[s][:, :, :], res_g[bass.ds(j * NS + (s + NS), 1)].rearrange("o p q c -> p (o q) c"))\
                        .then_inc(y2_loaded[s], 16)

        @block.scalar
        def _(act):
            act.dma_start(wg_sb[:, :], gnn_w).then_inc(small_loaded, 16)
            act.dma_start(vecs[0:E * HC, :], b1.rearrange("e (c p) -> (e c) p", p=P)).then_inc(small_loaded, 16)
            for n, v in enumerate((ln_g, ln_b, b2)):
                act.dma_start(vecs[E * HC + n * E:E * HC + (n + 1) * E, :], v).then_inc(small_loaded, 16)
            act.dma_start(bias_row[:, :, :], gnn_b.unsqueeze(0).unsqueeze(0).to_broadcast([1, Q, D])).then_inc(small_loaded, 16)
            act.dma_start(wr_sb[:, :], wr).then_inc(small_loaded, 16)
            act.dma_start(br_sb[:, :], br.partition_broadcast(P)).then_inc(small_loaded, 16)

            def norm_x(u, g):
                p = u[1] % 2
                ready = early(act, at(u, NORM, NORM))
                act.wait_ge(pool_const, 1)
                act.wait_ge(norm, ready)
                if not first(u):
                    used = early(act, at(off(u, -1), 2, g + 1))
                    act.wait_ge(pool_const, 1)
                    act.wait_ge(g_done, used)
                for q in range(Q):
                    t = g * Q + q
                    act.activation(xn[g][:, q, :], x_all[:, graph(u, g), q, :].rearrange("p o d -> p (o d)"), ACT.Identity,
                                   bias=shift[p][:, 1, t:t + 1], scale=rstd[p][:, 1, t:t + 1]).then_inc(xn_ready, 1)

            def norm_z(u):
                p = u[1] % 2
                ready = early(act, at(off(u, 2), NORM, NORM))
                act.wait_ge(pool_const, 1)
                act.wait_ge(norm, ready)
                if not first(u):
                    used = early(act, at(off(u, -1), 2, 2))
                    act.wait_ge(pool_const, 1)
                    act.wait_ge(z_turned, used)
                for t in range(UT):
                    g, q = divmod(t, Q)
                    act.activation(z[g][:, q, :], x_all[:, graph(u, g), q, :].rearrange("p o d -> p (o d)"), ACT.Identity,
                                   bias=shift[p][:, 0, t:t + 1], scale=rstd[p][:, 0, t:t + 1]).then_inc(z_ready, 1)

            def copy_adjT(u, g):
                if not first(u):
                    act.wait_ge(g_done, at(off(u, -1), 2, g + 1))
                for r in range(Q):
                    act.wait_ge(adj_turned, at(u, UT, g * Q + r + 1))
                    act.activation(adjT[g][:, r, :], psT[r % 2][:, :], ACT.Copy).then_inc(adjT_ready, 1)

            def copy_gT(u, g):
                if not first(u):
                    act.wait_ge(w_done, at(off(u, -1), 2, g + 1))
                act.wait_ge(g_done, at(u, 2, g + 1))
                act.activation(gT[g][:, :], psG[:, :], ACT.Copy).then_inc(gT_ready, 1)

            def copy_zT(u, g):
                if not first(u):
                    act.wait_ge(l_done, at(off(u, -1), 2, g + 1))
                act.wait_ge(z_turned, at(u, 2, g + 1))
                act.activation(zT[g][:, :], psZ[g][:, :], ACT.Copy).then_inc(zT_ready, 1)

            def exp_gap(u):
                act.wait_ge(route, at(u, ROUTE, 10))
                act.activation(e2[:, :], gap[:, :], ACT.Exp).then_inc(exp_ready, 1)

            def weights_hi(u):
                s = u[1] % 2
                e = cut(number(u, 2))
                ready = early(act, unit_slot(u, 32))
                scale = gcol[:, e]
                act.wait_ge(vecT_ready, 1)
                act.wait_ge(raw_in[s], ready)
                if not first(u):
                    used = early(act, at(off(u, -1), 2, 2))
                    act.wait_ge(vecT_ready, 1)
                    act.wait_ge(w_lo, used)
                act.activation(w1g[:, :], w1raw[s][:, :], ACT.Identity, scale=scale).then_inc(w_hi, 1)
                act.activation(w1pack[:, e, 0, :].rearrange("p o h -> p (o h)"), w1raw[s][:, :], ACT.Identity, scale=scale)\
                    .then_inc(w_hi, 1)
                act.activation(w2pack[:, e, 0, :].rearrange("p o h -> p (o h)"),
                               w2raw[s][:, :, :].rearrange("p c d -> p (c d)"), ACT.Copy).then_inc(w_hi, 1)

            def unit(u):
                if real_unit(u):
                    copy_gT(u, 0)
                    copy_adjT(u, 1)
                    weights_hi(u)
                if real_unit(off(u, -2)):
                    exp_gap(off(u, -2))
                if real_unit(off(u, -1)):
                    norm_z(off(u, -1))
                if real_unit(u):
                    copy_gT(u, 1)
                if real_unit(off(u, 1)):
                    copy_adjT(off(u, 1), 0)
                    norm_x(off(u, 1), 0)
                if real_unit(off(u, -1)):
                    copy_zT(off(u, -1), 0)
                    copy_zT(off(u, -1), 1)
                if real_unit(off(u, 1)):
                    norm_x(off(u, 1), 1)

            norm_x((None, 0), 0)
            norm_x((None, 0), 1)
            copy_adjT((None, 0), 0)
            walk(act, unit, 0, UNITS + 2, 2, UNITS - 2)

            def gelu(t):
                s, p = t[1] % NS, t[1] % 2
                if t[0] is not None or t[1] >= 2:
                    act.wait_ge(y_done, tat(off(t, -1), 1))
                for c in range(HC):
                    if t[0] is not None or t[1] >= 1:
                        used = early(act, tat(off(t, -1), 6, (1, 2, 4, 6)[c]))
                        act.wait_ge(vecT_ready, 1)
                        act.wait_ge(h_split, used)
                    act.wait_ge(h_done, tat(t, HC, c + 1))
                    act.activation(h[:, c, :], psH[c][:, :], ACT.Gelu, bias=bbuf[s][:, c:c + 1]).then_inc(gelu_done, 1)
                    if 1 <= c <= 2:
                        act.wait_ge(gelu_done, tat(t, HC, c))
                        act.activation(h_hi[p][:, c - 1, :], h[:, c - 1, :], ACT.Copy).then_inc(hi_done, 1)

            def copy_yT(t):
                if t[0] is not None or t[1] >= 1:
                    act.wait_ge(y_turned, tat(t, 1))
                act.wait_ge(y_done, tat(t, 1, 1))
                act.activation(yT[:, :], psY[:, :], ACT.Identity, bias=bbuf[t[1] % NS][:, HC:HC + 1]).then_inc(yT_ready, 1)

            act.wait_ge(table, 20)
            gelu((None, 0))

            def tile(t):
                if real_tile(off(t, 1)):
                    gelu(off(t, 1))
                copy_yT(t)

            walk_tiles(act, tile)

            for s in range(2):
                act.wait_ge(sum2, s + 1)
                act.dma_start(out_g[s], fin[s][:, :, :]).then_inc(stored[s], 16)
            with act.Fori(0, B // 2 - 1) as j:
                for s in range(2):
                    act.wait_ge(sum2, j * 2 + (2 + s + 1))
                    act.dma_start(out_g[bass.ds(j * 2 + (s + 2), 1)].rearrange("o p q d -> p (o q) d"), fin[s][:, :, :])\
                        .then_inc(stored[s], 16)
            for s in range(2):
                act.wait_ge(stored[s], B // 2 * 16)

        @block.tensor
        def _(pe):
            def turn_adj(u, g):
                pe.wait_ge(adj_loaded[g], at(u, 16, 16))
                for r in range(Q):
                    if not (first(u) and g == 0 and r < 2):
                        pe.wait_ge(adjT_ready, at(u, UT, g * Q + r - 1))
                    for q in range(Q):
                        last = nc.tensor.transpose(psT[r % 2][:, q * P:(q + 1) * P], adj_sb[g][:, q, r * P:(r + 1) * P], ident[:, :])
                    last.then_inc(adj_turned, 1)

            def aggregate(u, g):
                pe.wait_ge(xn_ready, at(u, UT, Q * (g + 1)))
                pe.wait_ge(adjT_ready, at(u, UT, Q * (g + 1)))
                if not (first(u) and g == 0):
                    pe.wait_ge(gT_ready, at(u, 2, g))
                for r in range(Q):
                    last = nc.tensor.matmul(psG[:, :], xn[g][:, r, :], adjT[g][:, r, :], start=(r == 0), stop=(r == Q - 1))
                last.then_inc(g_done, 1)

            def project(u, g):
                if not first(u):
                    pe.wait_ge(x1_ready, at(off(u, -1), 2, g + 1))
                nc.tensor.matmul(psO[g][:, :], ones_row[:, :], bias_row[:, :, :].rearrange("o q d -> o (q d)"), start=True, stop=False)
                pe.wait_ge(gT_ready, at(u, 2, g + 1))
                for q in range(Q):
                    last = nc.tensor.matmul(psO[g][:, q * D:(q + 1) * D], gT[g][:, q * P:(q + 1) * P], wg_sb[:, :],
                                            start=False, stop=(q == Q - 1))
                last.then_inc(w_done, 1)

            def turn_z(u, g):
                pe.wait_ge(z_ready, at(u, UT, Q * (g + 1)))
                if not first(u):
                    pe.wait_ge(zT_ready, at(off(u, -1), 2, g + 1))
                for q in range(Q):
                    last = nc.tensor.transpose(psZ[g][:, q * P:(q + 1) * P], z[g][:, q, :], ident[:, :])
                last.then_inc(z_turned, 1)

            def logits(u, g):
                pe.wait_ge(zT_ready, at(u, 2, g + 1))
                if not first(u) and g == 0:
                    pe.wait_ge(route, at(off(u, -1), ROUTE, 2))
                for q in range(Q):
                    last = nc.tensor.matmul(psL[:, g * Q + q, :], zT[g][:, q * P:(q + 1) * P], wr_sb[:, :], start=True, stop=True)
                if g == 1:
                    s = u[1] % 2
                    pe.wait_ge(raw_in[s], unit_slot(u, 32))
                    for c in range(HC):
                        last = nc.tensor.matmul(psB1[:, c:c + 1], w1raw[s][:, c * P:(c + 1) * P], bcol[:, cut(number(u, 2))],
                                                start=True, stop=True)
                last.then_inc(l_done, 1)

            def rank(u):
                pe.wait_ge(route, at(u, ROUTE, 15))
                nc.tensor.matmul(psR[:, :, :], before[:, :], sel[:, :, :], start=True, stop=False)
                nc.tensor.matmul(psR[:, :, :], ones[:, :], sel_before[:, :].unsqueeze(1).to_broadcast([P, UT, E]), start=False, stop=False)
                for t in range(UT - 1):
                    last = nc.tensor.matmul(psR[:, t + 1:UT, :], ones[:, :],
                                            sel[:, t:t + 1, :].to_broadcast([P, UT - 1 - t, E]), start=False, stop=(t == UT - 2))
                last.then_inc(rank_done, 1)

            def unit(u):
                if real_unit(u):
                    aggregate(u, 0)
                    turn_adj(u, 1)
                    project(u, 0)
                    aggregate(u, 1)
                if real_unit(off(u, -2)):
                    rank(off(u, -2))
                if real_unit(off(u, 1)):
                    turn_adj(off(u, 1), 0)
                if real_unit(u):
                    project(u, 1)
                if real_unit(off(u, -1)):
                    turn_z(off(u, -1), 0)
                    turn_z(off(u, -1), 1)
                    logits(off(u, -1), 0)
                    logits(off(u, -1), 1)

            pe.wait_ge(pool_const, POOL_CONST)
            pe.wait_ge(dve_const, 4)
            pe.wait_ge(small_loaded, SMALL)
            nc.tensor.transpose(psVec, vecs[:, :], ident[0:VR, 0:VR]).then_inc(vecs_turned, 1)
            turn_adj((None, 0), 0)
            pe.wait_ge(vecT_ready, 1)
            walk(pe, unit, 0, UNITS + 2, 2, UNITS - 2)
            pe.wait_ge(route, ROUTE * UNITS)
            nc.tensor.matmul(psCnt, ones[:, :], sel_before[:, :], start=True, stop=True).then_inc(counted, 1)

            def turn_x(t):
                s = t[1] % NS
                pe.wait_ge(xt_in[s], by_slot(t, 32, NS))
                if t[0] is not None or t[1] >= 1:
                    pe.wait_ge(x_split, tat(t, 2))
                for i in range(J):
                    last = nc.tensor.transpose(psX[:, i * P:(i + 1) * P], xt[s][:, i, 0:D], ident[:, :])
                last.then_inc(xt_turned, 1)

            def up(t):
                p = t[1] % 2
                pe.wait_ge(w1_in[p], by_slot(t, 16, 2))
                pe.wait_ge(x_split, tat(t, 2, 2))
                for c in range(HC):
                    if t[0] is not None or t[1] >= 1:
                        pe.wait_ge(gelu_done, tat(off(t, -1), HC, c + 1))
                    hi, lo = (w1buf[p][:, a, c * P:(c + 1) * P] for a in range(2))
                    nc.tensor.matmul(psH[c][:, :], hi, x_hi[p][:, :], start=True, stop=False)
                    nc.tensor.matmul(psH[c][:, :], hi, x_lo[p][:, :], start=False, stop=False)
                    nc.tensor.matmul(psH[c][:, :], lo, x_hi[p][:, :], start=False, stop=True).then_inc(h_done, 1)

            def down(t):
                p = t[1] % 2
                pe.wait_ge(w2_in[p], by_slot(t, 16, 2))
                if t[0] is not None or t[1] >= 1:
                    pe.wait_ge(yT_ready, tat(t, 1))
                for c in range(HC):
                    pe.wait_ge(h_split, tat(t, 6, (1, 2, 4, 6)[c]))
                    hi, lo = (w2buf[p][:, a, c * D:(c + 1) * D] for a in range(2))
                    nc.tensor.matmul(psY[:, :], hi, h_hi[p][:, c, :], start=(c == 0), stop=False)
                    nc.tensor.matmul(psY[:, :], hi, h_lo[p][:, c, :], start=False, stop=False)
                    last = nc.tensor.matmul(psY[:, :], lo, h_hi[p][:, c, :], start=False, stop=(c == HC - 1))
                last.then_inc(y_done, 1)

            def turn_y(t):
                pe.wait_ge(yT_ready, tat(t, 1, 1))
                if t[0] is not None or t[1] >= 1:
                    pe.wait_ge(ys_ready, tat(t, 2))
                for i in range(J):
                    last = nc.tensor.transpose(psYt[:, i * P:(i + 1) * P], yT[:, i * P:(i + 1) * P], ident[:, :])
                last.then_inc(y_turned, 1)

            pe.wait_ge(table, 2)
            turn_x((None, 0))
            up((None, 0))
            turn_x((None, 1))

            def tile(t):
                if real_tile(off(t, 1)):
                    up(off(t, 1))
                if real_tile(off(t, 2)):
                    turn_x(off(t, 2))
                if t[0] is not None or t[1] >= 1:
                    turn_y(off(t, -1))
                down(t)

            walk_tiles(pe, tile)
            turn_y((None, TILES - 1))

        @block.vector
        def _(dve):
            V = nc.vector
            V.memset(ones[:, :], 1.0).then_inc(dve_const, 1)
            V.memset(ones_row[:, :], 1.0).then_inc(dve_const, 1)
            V.memset(pad_tile[:, :, :], 0.0).then_inc(dve_const, 1)
            dve.wait_ge(dve_const, 3)
            V.memset(pad_tile[:, :, D:D + 1].bitcast(I32), NOWHERE).then_inc(dve_const, 1)
            V.memset(sel_before[:, :], 0.0).then_inc(dve_const, 1)
            V.memset(one8[:, :], 1.0).then_inc(dve_const, 1)
            V.memset(stats[:, :, :, :], 1.0).then_inc(dve_const, 1)
            dve.wait_ge(pool_const, POOL_CONST)
            V.tensor_scalar(region_of[:, :], iota_i[:, 0:E], float(REGION), None, ALU.mult).then_inc(dve_const, 1)
            V.tensor_scalar(prefer_low[:, :], iota_i[:, 0:E], -1.0, float(E), ALU.mult, ALU.add).then_inc(dve_const, 1)
            V.tensor_scalar(thr[:, :], iota_i[0:1, 0:MAXT], float(TILE), None, ALU.mult).then_inc(dve_const, 1)
            V.tensor_copy(tnum[:, :], iota_i[0:1, 0:TILES]).then_inc(dve_const, 1)
            V.tensor_scalar(tnum8[:, :], iota_i[0:1, 0:TILES], float(TILE), float(-DUMMY), ALU.mult, ALU.add).then_inc(dve_const, 1)
            dve.wait_ge(dve_const, DVE_CONST)

            def stats_of_x(n):
                p = n[1] % 2
                dve.wait_ge(x_in[p], unit_slot(n, 16))
                if n[0] is not None or n[1] >= 1:
                    seen = early(dve, at(off(n, -1), NORM, NORM))
                    dve.wait_ge(dve_const, DVE_CONST)
                    dve.wait_ge(norm, seen)
                for t in range(UT):
                    V.bn_stats(stats[:, 1, t, :], x_all[:, graph(n, t // Q), t % Q, :].rearrange("p o d -> p (o d)"))\
                        .then_inc(stats_x, 1)

            def stats_of_x1(u):
                both_in = early(dve, at(u, 2, 2))
                dve.wait_ge(dve_const, DVE_CONST)
                dve.wait_ge(x1_ready, both_in)
                for t in range(UT):
                    V.bn_stats(stats[:, 0, t, :], x_all[:, graph(u, t // Q), t % Q, :].rearrange("p o d -> p (o d)"))\
                        .then_inc(stats_x1, 1)

            def per_tile(ap):
                return ap[:, :].unsqueeze(2).to_broadcast([P, UT, E])

            def per_expert(ap):
                return ap[:, :].unsqueeze(1).to_broadcast([P, UT, E])

            def norms_and_choice(n, norms, choice):
                p = n[1] % 2
                u = off(n, -3)
                r = lambda k: at(n, NORM, k)
                c = lambda k: at(u, ROUTE, k)
                if norms:
                    if real_unit(off(n, -2)):
                        dve.wait_ge(stats_x1, at(off(n, -2), UT, UT))
                    if real_unit(n):
                        dve.wait_ge(stats_x, at(n, UT, UT))
                    V.tensor_tensor(dif[:, :, :], stats[:, :, :, 1], stats[:, :, :, 4], ALU.subtract).then_inc(norm, 1)
                    V.tensor_tensor(spr[:, :, :], stats[:, :, :, 2], stats[:, :, :, 5], ALU.add).then_inc(norm, 1)
                    V.tensor_tensor(tot[:, :, :], stats[:, :, :, 1], stats[:, :, :, 4], ALU.add).then_inc(norm, 1)
                if choice:
                    e = cut(number(u, 2))
                    dve.wait_ge(l_done, at(u, 2, 2))
                    V.tensor_tensor(lg[:, :, :], psL[:, :, :], per_expert(br_sb), ALU.add).then_inc(route, 1)
                    V.tensor_tensor(bpack[:, e, 0:HC].rearrange("p o c -> p (o c)"), psB1,
                                    vecT[:, cut(number(u, 2, HC), HC)], ALU.add).then_inc(route, 1)
                if norms:
                    dve.wait_ge(norm, r(1))
                    V.scalar_tensor_tensor(sq[:, :, :], dif[:, :, :], 0.25, dif[:, :, :], ALU.mult, ALU.mult).then_inc(norm, 1)
                if choice:
                    dve.wait_ge(route, c(1))
                    V.tensor_reduce(top1[:, :], lg[:, :, :], AX.X, ALU.max).then_inc(route, 1)
                if norms:
                    dve.wait_ge(norm, r(4))
                    V.scalar_tensor_tensor(var[:, :, :], spr[:, :, :], 1.0 / D, sq[:, :, :], ALU.mult, ALU.add).then_inc(norm, 1)
                if choice:
                    dve.wait_ge(route, c(3))
                    V.tensor_tensor(eq1[:, :, :], lg[:, :, :], per_tile(top1), ALU.is_equal).then_inc(route, 1)
                if norms:
                    dve.wait_ge(norm, r(5))
                    V.tensor_scalar(arg[:, 0:2, :], var[:, :, :], LN_EPS, None, ALU.add).then_inc(norm, 1)
                if choice:
                    dve.wait_ge(route, c(4))
                    V.tensor_tensor(kk1[:, :, :], eq1[:, :, :], per_expert(prefer_low), ALU.mult).then_inc(route, 1)
                if norms:
                    dve.wait_ge(norm, r(6))
                    V.scalar_tensor_tensor(arg[:, 2, :], arg[:, 0, :], LN_EPS, var[:, 0, :], ALU.mult, ALU.add).then_inc(norm, 1)
                if choice:
                    dve.wait_ge(route, c(5))
                    V.tensor_reduce(key1[:, :], kk1[:, :, :], AX.X, ALU.max).then_inc(route, 1)
                if norms:
                    dve.wait_ge(norm, r(7))
                    V.tensor_scalar(half_bits[:, :, :], arg[:, :, :].bitcast(I32), 1, None, ALU.logical_shift_right).then_inc(norm, 1)
                if choice:
                    dve.wait_ge(route, c(6))
                    V.tensor_tensor(onehot[:, 0, :, :], kk1[:, :, :], per_tile(key1), ALU.is_equal).then_inc(route, 1)
                if norms:
                    dve.wait_ge(norm, r(8))
                    V.tensor_scalar(guess[:, :, :].bitcast(I32), half_bits[:, :, :], -1.0, float(MAGIC), ALU.mult, ALU.add).then_inc(norm, 1)
                if choice:
                    dve.wait_ge(route, c(7))
                    V.scalar_tensor_tensor(lg2[:, :, :], onehot[:, 0, :, :], -BIG, lg[:, :, :], ALU.mult, ALU.add).then_inc(route, 1)
                if norms:
                    dve.wait_ge(norm, r(9))
                    V.tensor_tensor(newton_a[:, :, :], arg[:, :, :], guess[:, :, :], ALU.mult).then_inc(norm, 1)
                if choice:
                    dve.wait_ge(route, c(8))
                    V.tensor_reduce(top2[:, :], lg2[:, :, :], AX.X, ALU.max).then_inc(route, 1)
                if norms:
                    dve.wait_ge(norm, r(10))
                    V.scalar_tensor_tensor(newton_b[:, :, :], newton_a[:, :, :], -0.5, guess[:, :, :], ALU.mult, ALU.mult).then_inc(norm, 1)
                if choice:
                    dve.wait_ge(route, c(9))
                    V.tensor_tensor(gap[:, :], top2[:, :], top1[:, :], ALU.subtract).then_inc(route, 1)
                    V.tensor_tensor(eq2[:, :, :], lg2[:, :, :], per_tile(top2), ALU.is_equal).then_inc(route, 1)
                if norms:
                    dve.wait_ge(norm, r(11))
                    V.scalar_tensor_tensor(guess[:, :, :], newton_b[:, :, :], 1.5, guess[:, :, :], ALU.add, ALU.mult).then_inc(norm, 1)
                if choice:
                    dve.wait_ge(route, c(11))
                    V.tensor_tensor(kk2[:, :, :], eq2[:, :, :], per_expert(prefer_low), ALU.mult).then_inc(route, 1)
                if norms:
                    dve.wait_ge(norm, r(12))
                    V.tensor_tensor(newton_a[:, :, :], arg[:, :, :], guess[:, :, :], ALU.mult).then_inc(norm, 1)
                if choice:
                    dve.wait_ge(route, c(12))
                    V.tensor_reduce(key2[:, :], kk2[:, :, :], AX.X, ALU.max).then_inc(route, 1)
                if norms:
                    dve.wait_ge(norm, r(13))
                    V.scalar_tensor_tensor(newton_b[:, :, :], newton_a[:, :, :], -0.5, guess[:, :, :], ALU.mult, ALU.mult).then_inc(norm, 1)
                if choice:
                    dve.wait_ge(route, c(13))
                    V.tensor_tensor(onehot[:, 1, :, :], kk2[:, :, :], per_tile(key2), ALU.is_equal).then_inc(route, 1)
                if norms:
                    dve.wait_ge(norm, r(14))
                    V.scalar_tensor_tensor(guess[:, :, :], newton_b[:, :, :], 1.5, guess[:, :, :], ALU.add, ALU.mult).then_inc(norm, 1)
                if choice:
                    dve.wait_ge(route, c(14))
                    V.tensor_tensor(sel[:, :, :], onehot[:, 0, :, :], onehot[:, 1, :, :], ALU.add).then_inc(route, 1)
                if norms:
                    dve.wait_ge(norm, r(15))
                    V.tensor_tensor(newton_a[:, :, :], arg[:, :, :], guess[:, :, :], ALU.mult).then_inc(norm, 1)
                if norms:
                    dve.wait_ge(norm, r(16))
                    V.scalar_tensor_tensor(newton_b[:, :, :], newton_a[:, :, :], -0.5, guess[:, :, :], ALU.mult, ALU.mult).then_inc(norm, 1)
                if norms:
                    dve.wait_ge(norm, r(17))
                    V.scalar_tensor_tensor(rstd[p][:, :, :], newton_b[:, :, :], 1.5, guess[:, :, :], ALU.add, ALU.mult).then_inc(norm, 1)
                if norms:
                    V.tensor_scalar(mean2[p][:, :], tot[:, 0, :], 0.5, None, ALU.mult).then_inc(norm, 1)
                    dve.wait_ge(norm, r(18))
                    V.scalar_tensor_tensor(shift[p][:, :, :], tot[:, :, :], -0.5, rstd[p][:, 0:2, :], ALU.mult, ALU.mult).then_inc(norm, 1)

            def residual(u, g):
                dve.wait_ge(w_done, at(u, 2, g + 1))
                xs = x_all[:, graph(u, g), :, :].rearrange("p o q d -> p (o q d)")
                V.tensor_tensor(xs, psO[g][:, :], xs, ALU.add).then_inc(x1_ready, 1)

            def make_rows(u):
                p = u[1] % 2
                dve.wait_ge(norm, at(off(u, 2), NORM, NORM - 1))
                dve.wait_ge(rows_free, at(u, 1, 1))
                for t in range(UT):
                    V.tensor_scalar(rows[p][:, t, :, 0:D], x_all[:, graph(u, t // Q), t % Q, :].to_broadcast([P, K, D]),
                                    mean2[p][:, t:t + 1], rstd[p][:, 2, t:t + 1], ALU.subtract, ALU.mult).then_inc(rows_ready, 1)
                idx = rows[p][:, :, :, D:D + 1].bitcast(I32)
                V.tensor_scalar(idx, idx, 4.0 * N * K, None, ALU.add).then_inc(rows_ready, 1)

            def assign(u):
                p = u[1] % 2
                r = lambda k: at(u, ROUTE, k)
                dve.wait_ge(exp_ready, at(u, 1, 1))
                V.tensor_scalar(den[:, :], e2[:, :], 1.0, None, ALU.add).then_inc(route, 1)
                dve.wait_ge(route, r(16))
                V.reciprocal(rows[p][:, :, 0, D + 1], den[:, :]).then_inc(route, 1)
                dve.wait_ge(route, r(17))
                V.tensor_tensor(rows[p][:, :, 1, D + 1], rows[p][:, :, 0, D + 1], e2[:, :], ALU.mult).then_inc(route, 1)
                dve.wait_ge(rank_done, at(u, 1, 1))
                V.tensor_tensor(pos[:, :, :], psR[:, :, :], per_expert(region_of), ALU.add).then_inc(route, 1)
                dve.wait_ge(route, r(19))
                for k in range(K):
                    V.tensor_tensor(place[:, k, :, :], onehot[:, k, :, :], pos[:, :, :], ALU.mult).then_inc(route, 1)
                dve.wait_ge(route, r(21))
                with nc.allow_low_precision(reason="a sum of one whole number below 2^24 and zeros"):
                    V.tensor_reduce(slot[p][:, :, :], place[:, :, :, :], AX.X, ALU.add).then_inc(route, 1)
                V.tensor_reduce(sel_sum[:, :], sel[:, :, :].rearrange("p t e -> p e t"), AX.X, ALU.add).then_inc(route, 1)
                dve.wait_ge(route, r(23))
                V.tensor_tensor(sel_before[:, :], sel_before[:, :], sel_sum[:, :], ALU.add).then_inc(route, 1)

            def weights_lo(u):
                s = u[1] % 2
                e = cut(number(u, 2))
                dve.wait_ge(w_hi, at(u, 3, 3))
                V.tensor_tensor(w1pack[:, e, 1, :].rearrange("p o h -> p (o h)"), w1g[:, :],
                                w1pack[:, e, 0, :].rearrange("p o h -> p (o h)").bitcast(FP32), ALU.subtract).then_inc(w_lo, 1)
                V.tensor_tensor(w2pack[:, e, 1, :].rearrange("p o h -> p (o h)"), w2raw[s][:, :, :].rearrange("p c d -> p (c d)"),
                                w2pack[:, e, 0, :].rearrange("p o h -> p (o h)").bitcast(FP32), ALU.subtract).then_inc(w_lo, 1)

            def unit(u):
                if real_unit(off(u, 1)):
                    stats_of_x(off(u, 1))
                if real_unit(off(u, -1)):
                    residual(off(u, -1), 1)
                    stats_of_x1(off(u, -1))
                norms_and_choice(off(u, 1), u[0] is not None or u[1] <= UNITS, real_unit(off(u, -2)))
                if real_unit(off(u, -2)):
                    make_rows(off(u, -2))
                if real_unit(u):
                    residual(u, 0)
                if real_unit(off(u, -2)):
                    assign(off(u, -2))
                if real_unit(u):
                    weights_lo(u)

            stats_of_x((None, 0))
            norms_and_choice((None, 0), True, False)
            dve.wait_ge(small_loaded, SMALL)
            dve.wait_ge(vecs_turned, 1)
            V.tensor_copy(vecT[:, :], psVec).then_inc(vecT_ready, 1)
            dve.wait_ge(vecT_ready, 1)
            V.tensor_copy(bpack[:, :, HC], b2col).then_inc(vecT_ready, 1)
            walk(dve, unit, 0, UNITS + 2, 2, UNITS - 2)

            n = [0]

            def step(ins):
                n[0] += 1
                ins.then_inc(table, 1)
                dve.wait_ge(table, n[0])

            te = [1, TILES, E]
            dve.wait_ge(counted, 1)
            step(V.tensor_copy(cnt[:, :], psCnt[0:1, :]))
            step(V.tensor_tensor(base_row[:, :], cnt[:, :], region_of[0:1, :], ALU.add))
            step(V.tensor_copy(tab_pad[:, :], base_row[:, :]))
            step(V.tensor_tensor(more[:, :, :], cnt[:, :].unsqueeze(2).to_broadcast([1, E, MAXT]),
                                 thr[:, :].unsqueeze(1).to_broadcast([1, E, MAXT]), ALU.is_gt))
            step(V.tensor_reduce(nt[:, :], more[:, :, :], AX.X, ALU.add))
            step(V.tensor_tensor_scan(t_end[:, :], one8[:, :], nt[:, :], 0.0, ALU.mult, ALU.add))
            step(V.tensor_tensor(t_start[:, :], t_end[:, :], nt[:, :], ALU.subtract))
            step(V.tensor_tensor(ge_end[:, :, :], tnum[:, :].unsqueeze(2).to_broadcast(te), t_end[:, :].unsqueeze(1).to_broadcast(te), ALU.is_ge))
            step(V.tensor_tensor(ge_start[:, :, :], tnum[:, :].unsqueeze(2).to_broadcast(te), t_start[:, :].unsqueeze(1).to_broadcast(te), ALU.is_ge))
            step(V.tensor_tensor(mine[:, :, :], ge_start[:, :, :], ge_end[:, :, :], ALU.subtract))
            step(V.tensor_reduce(eid[:, :], ge_end[:, :, :], AX.X, ALU.add))
            step(V.tensor_scalar(tab_e[:, :], eid[:, :], float(E - 1), None, ALU.min))
            step(V.tensor_reduce(real[:, :], mine[:, :, :], AX.X, ALU.add))
            step(V.scalar_tensor_tensor(base_row[:, :], t_start[:, :], float(-TILE), region_of[0:1, :], ALU.mult, ALU.add))
            step(V.tensor_tensor(mine_row[:, :, :], mine[:, :, :], base_row[:, :].unsqueeze(1).to_broadcast(te), ALU.mult))
            step(V.tensor_reduce(row_a[:, :], mine_row[:, :, :], AX.X, ALU.add))
            step(V.tensor_tensor(row_b[:, :], real[:, :], tnum8[:, :], ALU.mult))
            step(V.tensor_tensor(row_a[:, :], row_a[:, :], row_b[:, :], ALU.add))
            step(V.tensor_scalar(row_b[:, :], row_a[:, :], float(DUMMY), None, ALU.add))
            step(V.tensor_copy(tab_row[:, :], row_b[:, :]))

            def split_x(t):
                p = t[1] % 2
                if t[0] is not None or t[1] >= 2:
                    dve.wait_ge(h_done, tat(off(t, -1), HC))
                dve.wait_ge(xt_turned, tat(t, 1, 1))
                V.tensor_copy(x_hi[p][:, :], psX[:, :]).then_inc(x_split, 1)
                dve.wait_ge(x_split, tat(t, 2, 1))
                V.tensor_tensor(x_lo[p][:, :], psX[:, :], x_hi[p][:, :].bitcast(FP32), ALU.subtract).then_inc(x_split, 1)

            def split_h(t, c):
                p = t[1] % 2
                if c == 0 and (t[0] is not None or t[1] >= 2):
                    dve.wait_ge(y_done, tat(off(t, -1), 1))
                if c < 2:
                    dve.wait_ge(hi_done, tat(t, 2, c + 1))
                else:
                    dve.wait_ge(gelu_done, tat(t, HC, c + 1))
                    V.tensor_copy(h_hi[p][:, c, :], h[:, c, :]).then_inc(h_split, 1)
                    dve.wait_ge(h_split, tat(t, 6, (3, 5)[c - 2]))
                V.tensor_tensor(h_lo[p][:, c, :], h[:, c, :], h_hi[p][:, c, :].bitcast(FP32), ALU.subtract).then_inc(h_split, 1)

            def finish(t):
                s, p = t[1] % NS, t[1] % 2
                if t[0] is not None or t[1] >= 2:
                    dve.wait_ge(y_scattered[p], by_slot(off(t, -2), J * 16, 2))
                V.tensor_copy(result_row[p][:, :], xt[s][:, :, D:D + 1].bitcast(I32).rearrange("p j o -> p (j o)"))\
                    .then_inc(ys_ready, 1)
                dve.wait_ge(y_turned, tat(t, 1, 1))
                V.tensor_tensor(ys[p][:, :, :], psYt[:, :].rearrange("p (j d) -> p j d", j=J),
                                xt[s][:, :, D + 1:D + 2].to_broadcast([P, J, D]), ALU.mult).then_inc(ys_ready, 1)

            split_x((None, 0))
            split_h((None, 0), 0)
            split_x((None, 1))
            for c in range(1, HC):
                split_h((None, 0), c)

            def tile(t):
                if real_tile(off(t, 1)):
                    split_h(off(t, 1), 0)
                if real_tile(off(t, 2)):
                    split_x(off(t, 2))
                if real_tile(off(t, 1)):
                    split_h(off(t, 1), 1)
                if t[0] is not None or t[1] >= 1:
                    finish(off(t, -1))
                if real_tile(off(t, 1)):
                    split_h(off(t, 1), 2)
                    split_h(off(t, 1), 3)

            walk_tiles(dve, tile)
            finish((None, TILES - 1))

            def combine(j, s, g0):
                f = (s + g0) % 2
                xs = x_all[:, cut(s + g0 if j is None else j * NS + (s + g0)), :, :].rearrange("p o q d -> p (o q) d")
                dve.wait_ge(y2_loaded[s], 16 if j is None else j * 16 + 32)
                V.tensor_tensor(xs, xs, y2[s][:, :, 0:D], ALU.add).then_inc(sum1, 1)
                if j is not None or s >= 2:
                    dve.wait_ge(stored[f], s // 2 * 16 if j is None else j * 32 + (s // 2 + 2) * 16)
                dve.wait_ge(sum1, s + 1 if j is None else j * NS + (NS + s + 1))
                V.tensor_tensor(fin[f][:, :, :], xs, y2[s][:, :, D:2 * D], ALU.add).then_inc(sum2, 1)

            for s in range(NS):
                combine(None, s, 0)
            with dve.Fori(0, B // NS - 1) as j:
                for s in range(NS):
                    combine(j, s, NS)

        @block.gpsimd
        def _(pool):
            G = nc.gpsimd
            G.memset(ident[:, :], 0.0).then_inc(pool_const, 1)
            G.memset(before[:, :], 0.0).then_inc(pool_const, 1)
            pool.wait_ge(pool_const, 2)
            G.affine_select(out=ident[:, :], in_=ident[:, :], compare_op=ALU.not_equal, fill=1.0, base=0,
                            pattern=[[-1, P]], channel_multiplier=1).then_inc(pool_const, 1)
            G.affine_select(out=before[:, :], in_=before[:, :], compare_op=ALU.is_ge, fill=1.0, base=0,
                            pattern=[[-1, P]], channel_multiplier=1).then_inc(pool_const, 1)
            G.iota(iota_i[:, :], pattern=[[1, 64]], base=0, channel_multiplier=0).then_inc(pool_const, 1)
            for u in range(2):
                idx = rows[u][:, :, :, D:D + 1].bitcast(I32).rearrange("p t k o -> p t (k o)")
                G.iota(idx, pattern=[[K * P, UT], [1, K]], base=K * 2 * N * (u - 2), channel_multiplier=K).then_inc(pool_const, 1)
            pool.sem_inc(rows_free, 2)

            def scatter(u):
                p = u[1] % 2
                slots_in = early(pool, at(u, ROUTE, 22))
                pool.wait_ge(pool_const, POOL_CONST)
                pool.wait_ge(route, slots_in)
                for t in range(UT):
                    for k in range(K):
                        G.indirect_dma_start(out=sorted_rows, out_offset=bass.IndirectOffsetOnAxis(ap=slot[p][:, k, t:t + 1], axis=0),
                                             in_=rows[p][:, t, k, :], in_offset=None,
                                             bounds_check=DUMMY - 1, oob_is_err=False).then_inc(scattered[p], 16)
                    if t == 2 and (u[0] is not None or u[1] >= 1):
                        pool.wait_ge(scattered[1 - p], unit_slot(off(u, -1), UT * K * 16))
                        pool.sem_inc(rows_free, 1)

            scatter((None, 0))
            with pool.Fori(0, UNITS // 2 - 1) as j:
                scatter((j, 1))
                scatter((j, 2))
            scatter((None, UNITS - 1))

            def send(t):
                p = t[1] % 2
                both_in = early(pool, tat(t, 2, 2))
                pool.wait_ge(pool_const, POOL_CONST)
                pool.wait_ge(ys_ready, both_in)
                for i in range(J):
                    G.indirect_dma_start(out=result_rows,
                                         out_offset=bass.IndirectOffsetOnAxis(ap=result_row[p][:, i:i + 1], axis=0),
                                         in_=ys[p][:, i, :], in_offset=None,
                                         bounds_check=TOK * K - 1, oob_is_err=False).then_inc(y_scattered[p], 16)

            walk_tiles(pool, send)


_INS = ['x', 'adj', 'L0_gnn_weight', 'L0_gnn_bias', 'L0_ffn_Wr', 'L0_ffn_br', 'L0_ffn_ln_g', 'L0_ffn_ln_b',
        'L0_ffn_W1', 'L0_ffn_b1', 'L0_ffn_W2', 'L0_ffn_b2']


def kernel(**inputs):
    import numpy as _np
    import concourse.bacc as _bacc
    from concourse import mybir as _mybir
    from concourse.bass_utils import run_bass_kernel_spmd as _run

    nc = _bacc.Bacc("TRN2", target_bir_lowering=False, num_devices=1)
    arrays, args = {}, []
    for name in _INS:
        a = _np.ascontiguousarray(inputs[name])
        arrays[f"in_{name}_dram"] = a
        args.append(nc.dram_tensor(f"in_{name}_dram", a.shape, _mybir.dt.from_np(a.dtype), kind="ExternalInput").ap())
    out = nc.dram_tensor("out_dram", arrays["in_x_dram"].shape, _mybir.dt.float32, kind="ExternalOutput").ap()
    build(nc, *args, out)
    r = _run(nc, [arrays], core_ids=[0])
    return r.results[0]["out_dram"]
```

```python
import concourse.bass as bass
from concourse import mybir
from contextlib import ExitStack

FP32 = mybir.dt.float32
FP32R = mybir.dt.float32r
BF16 = mybir.dt.bfloat16
I32 = mybir.dt.int32
ALU = mybir.AluOpType
ACT = mybir.ActivationFunctionType
AX = mybir.AxisListType

P = 128
J = 4
TILE = J * P
LN_EPS = 1e-5
BIG = 3.0e38


def build(nc, x, adj, gnn_w, gnn_b, wr, br, ln_g, ln_b, w1, b1, w2, b2, out):
    B, N, D = x.shape
    E = wr.shape[1]
    H = w1.shape[2]
    Q = N // P
    HC = H // P
    K = 2
    TOK = B * N
    UNITS = B // 2
    UT = 2 * Q
    TILES = (TOK * K - E) // TILE + E
    REGION = TOK + TILE
    DUMMY = E * REGION
    RW = D + 2
    BW = HC + 1
    NS = 6
    MAXT = TOK // TILE
    MAGIC = 0x5F3759DF

    ctx = ExitStack()
    with ctx:
        def sb(name, shape, dt=FP32, stack=ctx):
            return stack.enter_context(nc.sbuf_tensor(name, shape, dt))

        def sem(name):
            return ctx.enter_context(nc.semaphore(name))

        sorted_rows = nc.dram_tensor("sorted_rows", [DUMMY + 2 * TILE, RW], FP32, kind="Internal").ap()

        ident = sb("ident", [P, P])
        before = sb("before", [P, P], BF16)
        ones = sb("ones", [P, P], BF16)
        ones_row = sb("ones_row", [1, P], FP32R)
        warm = sb("warm", [P, 1])
        prefer_low = sb("prefer_low", [P, E])
        region_of = sb("region_of", [P, E])
        iota_i = sb("iota_i", [P, 64], I32)
        wg_sb = sb("wg_sb", [P, D])
        wr_sb = sb("wr_sb", [P, E])
        br_sb = sb("br_sb", [P, E])
        VR = E * HC + 3 * E
        vecs = sb("vecs", [VR, P])
        vecT = sb("vecT", [P, VR])
        gcol = vecT[:, E * HC:E * HC + E]
        bcol = vecT[:, E * HC + E:E * HC + 2 * E]
        b2col = vecT[:, E * HC + 2 * E:VR]
        pad_tile = [sb(f"pad_tile{k}", [P, J, RW]) for k in range(2)]

        x_all = sb("x_all", [P, B, Q, D])
        w1pack = sb("w1pack", [P, E, 2, H], FP32R)
        w2pack = sb("w2pack", [P, E, 2, HC * D], FP32R)
        bpack = sb("bpack", [P, E, BW])
        tab_e = sb("tab_e", [1, TILES], I32)
        tab_row = sb("tab_row", [1, TILES], I32)
        tab_pad = sb("tab_pad", [1, E], I32)
        tab_land = sb("tab_land", [1, TILES], I32)

        EARLY = 3
        tab_late = sb("tab_late", [1, EARLY], I32)
        last_rows = sb("last_rows", [P, UT, K, RW])
        last_slot = sb("last_slot", [P, K, UT], I32)
        rstd = [sb(f"rstd{u}", [P, 3, UT]) for u in range(2)]
        mean2 = [sb(f"mean2_{u}", [P, UT]) for u in range(2)]

        part_a = ExitStack()
        def sa(name, shape, dt=FP32):
            return sb(name, shape, dt, part_a)
        adj_sb = [sa(f"adj_sb{g}", [P, Q, N]) for g in range(2)]
        adjT = [sa(f"adjT{g}", [P, Q, N]) for g in range(2)]
        xn = [sa(f"xn{g}", [P, Q, D]) for g in range(2)]
        gT = [sa(f"gT{g}", [P, N]) for g in range(2)]
        z = [sa(f"z{g}", [P, Q, D]) for g in range(2)]
        zT = [sa(f"zT{g}", [P, N]) for g in range(2)]
        w1raw = [sa(f"w1raw{s}", [P, H]) for s in range(2)]
        w2raw = [sa(f"w2raw{s}", [P, HC, D]) for s in range(2)]
        w1g = sa("w1g", [P, H])
        stats = sa("stats", [P, 2, UT, 6])
        dif, spr, tot, sq, var = (sa(n, [P, 2, UT]) for n in ("dif", "spr", "tot", "sq", "var"))
        arg = sa("arg", [P, 3, UT])
        half_bits = sa("half_bits", [P, 3, UT], I32)
        guess = sa("guess", [P, 3, UT])
        newton_a = sa("newton_a", [P, 3, UT])
        newton_b = sa("newton_b", [P, 3, UT])
        shift = [sa(f"shift{u}", [P, 2, UT]) for u in range(2)]
        rows = [sa("rows0", [P, UT, K, RW]), last_rows]
        slot = [sa("slot0", [P, K, UT], I32), last_slot]
        lg = sa("lg", [P, UT, E])
        lg2 = sa("lg2", [P, UT, E])
        top1, top2, gap, key1, key2, e2, den = (
            sa(n, [P, UT]) for n in ("top1", "top2", "gap", "key1", "key2", "e2", "den"))
        eq1, eq2, kk1, kk2, pos = (sa(n, [P, UT, E]) for n in ("eq1", "eq2", "kk1", "kk2", "pos"))
        onehot = sa("onehot", [P, K, UT, E])
        sel = sa("sel", [P, UT, E], BF16)
        place = sa("place", [P, K, UT, E])
        sel_sum = sa("sel_sum", [P, E])
        sel_before = sa("sel_before", [P, E], BF16)
        cnt, nt, one8, t_end, t_start, base_row = (
            sa(n, [1, E]) for n in ("cnt", "nt", "one8", "t_end", "t_start", "base_row"))
        thr = sa("thr", [1, MAXT])
        more = sa("more", [1, E, MAXT])
        tnum, row_less, eid, real, row_a, row_b, row_c, row_d = (
            sa(n, [1, TILES]) for n in ("tnum", "row_less", "eid", "real", "row_a", "row_b", "row_c", "row_d"))
        cnt_early, early_end, row_start = (sa(n, [1, E]) for n in ("cnt_early", "early_end", "row_start"))
        mine_early, tile_early = sa("mine_early", [1, EARLY, E]), sa("tile_early", [1, EARLY])
        land_i = sa("land_i", [1, 2 * (TILES // 2 + 1)], I32)
        dummy_i = sa("dummy_i", [1, 2 * (TILES // 2 + 1)], I32)
        last_land, same, dummy_row = (sa(n, [1, TILES]) for n in ("last_land", "same", "dummy_row"))
        ge_end, ge_start, mine, mine_row = (
            sa(n, [1, TILES, E]) for n in ("ge_end", "ge_start", "mine", "mine_row"))
        bias_row = sa("bias_row", [1, Q * D])
        bias_hi = sa("bias_hi", [1, Q * D], FP32R)
        bias_lo = sa("bias_lo", [1, Q * D], FP32R)
        part_a.close()

        w1buf = [sb(f"w1buf{s}", [P, 2, H], FP32R) for s in range(2)]
        w2buf = [sb(f"w2buf{s}", [P, 2, HC * D], FP32R) for s in range(2)]
        bbuf = [sb(f"bbuf{s}", [P, BW]) for s in range(NS)]
        xt = [sb(f"xt{s}", [P, J, RW]) for s in range(NS)]
        x_hi = [sb(f"x_hi{s}", [P, TILE], FP32R) for s in range(2)]
        x_lo = [sb(f"x_lo{s}", [P, TILE], FP32R) for s in range(2)]
        h = sb("h", [P, HC, TILE])
        h_hi = [sb(f"h_hi{s}", [P, HC, TILE], FP32R) for s in range(2)]
        h_lo = [sb(f"h_lo{s}", [P, HC, TILE], FP32R) for s in range(2)]
        yT = sb("yT", [P, TILE])
        ys = [sb(f"ys{s}", [P, J, D]) for s in range(2)]
        result_row = [sb(f"result_row{s}", [P, J], I32) for s in range(2)]

        bank = [ctx.enter_context(nc.psum_tensor(f"bank{i}", [P, 512], FP32)) for i in range(8)]
        psT = [bank[0], bank[1]]
        psG = bank[2]
        psO = [bank[3], bank[4]]
        psZ = bank[5]
        psL = bank[6][:, 0:UT * E].rearrange("p (t e) -> p t e", e=E)
        psR = bank[7][:, 0:UT * E].rearrange("p (t e) -> p t e", e=E)
        psCnt = bank[7][:, UT * E:UT * E + E]
        psB1 = bank[7][:, 128:128 + HC]
        psEarly = bank[7][:, 256:256 + E]
        psVec = bank[6][:, 384:384 + VR]
        psH = [bank[c] for c in range(HC)]
        psX = bank[4]
        psY = bank[5]
        psYt = bank[6]

        x_in = [sem(f"x_in{s}") for s in range(2)]
        small_loaded = sem("small_loaded")
        vecs_loaded = sem("vecs_loaded")
        bias_split = sem("bias_split")
        adj_loaded = [sem(f"adj_loaded{g}") for g in range(2)]
        raw_in = [sem(f"raw_in{s}") for s in range(2)]
        pool_const = sem("pool_const")
        dve_const = sem("dve_const")
        table_in = sem("table_in")
        vecs_turned = sem("vecs_turned")
        vecT_ready = sem("vecT_ready")
        padding = sem("padding")
        stats_x = sem("stats_x")
        stats_x1 = sem("stats_x1")
        norm = sem("norm")
        z_ready = sem("z_ready")
        xn_ready = sem("xn_ready")
        adj_turned = sem("adj_turned")
        adjT_ready = sem("adjT_ready")
        g_done = sem("g_done")
        gT_ready = sem("gT_ready")
        w_done = sem("w_done")
        x1_ready = sem("x1_ready")
        z_turned = sem("z_turned")
        zT_ready = sem("zT_ready")
        l_done = sem("l_done")
        b1_done = sem("b1_done")
        b1_ready = sem("b1_ready")
        rows_ready = sem("rows_ready")
        route = sem("route")
        exp_ready = sem("exp_ready")
        rank_done = sem("rank_done")
        w_hi = sem("w_hi")
        w_lo = sem("w_lo")
        scattered = [sem(f"scattered{u}") for u in range(2)]
        rows_free = sem("rows_free")
        counted = sem("counted")
        early_copied = sem("early_copied")
        table = sem("table")
        w1_in = [sem(f"w1_in{s}") for s in range(2)]
        w2_in = [sem(f"w2_in{s}") for s in range(2)]
        xt_in = [sem(f"xt_in{s}") for s in range(NS)]
        xt_turned = sem("xt_turned")
        x_split = sem("x_split")
        h_done = sem("h_done")
        gelu_done = sem("gelu_done")
        hi_done = sem("hi_done")
        h_split = sem("h_split")
        y_done = sem("y_done")
        yT_ready = sem("yT_ready")
        y_turned = sem("y_turned")
        ys_ready = sem("ys_ready")
        y_scattered = [sem(f"y_scattered{s}") for s in range(2)]
        x1_stored = sem("x1_stored")
        zeros_stored = sem("zeros_stored")

        SMALL = 4 * 16
        VECS = 4 * 16
        NORM = 20
        ROUTE = 23
        TABLE = 26
        POOL_CONST = 11
        DVE_CONST = 15

        def at(u, per, k=0, step=2):
            j, b = u
            return per * b + k if j is None else j * (step * per) + (per * b + k)

        def tat(t, per, k=0):
            return at(t, per, k, NS)

        def by_slot(t, per, slots):
            j, b = t
            r = per * (b // slots + 1)
            return r if j is None else j * (NS // slots * per) + r

        def unit_slot(u, per):
            j, b = u
            r = per * (b // 2 + 1)
            return r if j is None else j * per + r

        def off(u, d):
            return (u[0], u[1] + d)

        def number(u, step, scale=1, add=0):
            j, b = u
            n = scale * b + add
            return n if j is None else j * (step * scale) + n

        def cut(n, size=1):
            return slice(n, n + size) if isinstance(n, int) else bass.ds(n, size)

        def graph(u, g):
            return cut(number(u, 2, 2, g))

        def real_unit(u):
            return u[0] is not None or 0 <= u[1] < UNITS

        def first(u):
            return u[0] is None and u[1] == 0

        def early(eng, value):
            return value if isinstance(value, int) else eng.snap(eng.to_reg(value))

        def walk(eng, body, lo, hi, loop_lo, loop_hi):
            for b in range(lo, loop_lo):
                body((None, b))
            with eng.Fori(0, (loop_hi - loop_lo) // 2) as j:
                body((j, loop_lo))
                body((j, loop_lo + 1))
            for b in range(loop_hi, hi):
                body((None, b))

        HEAD = NS
        TURNS = (TILES - 2 * NS + 1) // NS

        def walk_tiles(eng, body):
            for b in range(HEAD):
                body((None, b))
            with eng.Fori(0, TURNS) as j:
                for b in range(NS):
                    body((j, HEAD + b))
            for b in range(HEAD + NS * TURNS, TILES):
                body((None, b))

        def real_tile(t):
            return t[0] is not None or 0 <= t[1] < TILES

        block = ctx.enter_context(nc.Block())

        x_g = x.rearrange("b (q p) d -> p b q d", p=P)
        adj_g = adj.rearrange("b (q p) m -> b p q m", p=P)
        out_g = out[0:TOK, :].rearrange("(b q p) d -> p b q d", q=Q, p=P)

        @block.sync
        def _(sp):
            def load_x(u):
                j, b = u
                if j is None:
                    src = x_g[:, 2 * b:2 * b + 2]
                else:
                    src = x_g[:, bass.ds(number(u, 2, 2), 2)]
                sp.dma_start(x_all[:, cut(number(u, 2, 2), 2)], src).then_inc(x_in[b % 2], 16)

            def load_adj(u, g):
                if not first(u):
                    sp.wait_ge(adj_turned, at(off(u, -1), UT, Q * g + Q))
                sp.dma_start(adj_sb[g][:, :, :], adj_g[cut(number(u, 2, 2, g))].rearrange("o p q m -> p (o q) m"))\
                    .then_inc(adj_loaded[g], 16)

            def load_raw(u):
                s = u[1] % 2
                if u[0] is not None or u[1] >= 2:
                    used_b1 = early(sp, at(off(u, -2), 1, 1))
                    sp.wait_ge(w_lo, at(off(u, -2), 2, 2))
                    sp.wait_ge(b1_done, used_b1)
                e = cut(number(u, 2))
                sp.dma_start(w1raw[s][:, :], w1[e].rearrange("o d h -> d (o h)")).then_inc(raw_in[s], 16)
                sp.dma_start(w2raw[s][:, :, :], w2[e].rearrange("o (c p) d -> p (o c) d", p=P)).then_inc(raw_in[s], 16)

            def store_x1(u):
                graphs = cut(number(u, 2, 2), 2)
                sp.dma_start(out_g[:, graphs], x_all[:, graphs]).then_inc(x1_stored, 16)

            load_x((None, 0))
            load_adj((None, 0), 0)
            sp.dma_start(wg_sb[:, :], gnn_w).then_inc(small_loaded, 16)
            sp.dma_start(bias_row[:, :].rearrange("o (q d) -> o q d", d=D), gnn_b.unsqueeze(0).unsqueeze(0).to_broadcast([1, Q, D])).then_inc(small_loaded, 16)
            sp.dma_start(wr_sb[:, :], wr).then_inc(small_loaded, 16)
            sp.dma_start(br_sb[:, :], br.partition_broadcast(P)).then_inc(small_loaded, 16)
            sp.dma_start(vecs[0:E * HC, :], b1.rearrange("e (c p) -> (e c) p", p=P)).then_inc(vecs_loaded, 16)
            for n, v in enumerate((ln_g, ln_b, b2)):
                sp.dma_start(vecs[E * HC + n * E:E * HC + (n + 1) * E, :], v).then_inc(vecs_loaded, 16)
            load_adj((None, 0), 1)
            load_x((None, 1))
            load_raw((None, 0))
            load_raw((None, 1))
            sp.wait_ge(dve_const, 4)
            sp.wait_ge(pool_const, POOL_CONST)
            for k in range(2):
                sp.dma_start(out[TOK + k * TILE:TOK + (k + 1) * TILE, :].rearrange("(p j) d -> p j d", j=J), pad_tile[k][:, :, 0:D])\
                    .then_inc(zeros_stored, 16)
                sp.dma_start(sorted_rows[DUMMY + k * TILE:DUMMY + (k + 1) * TILE, :].rearrange("(p j) c -> p (j c)", j=J),
                             pad_tile[k][:, :, :].rearrange("p j c -> p (j c)")).then_inc(padding, 16)

            def unit(u):
                if real_unit(off(u, 1)):
                    load_adj(off(u, 1), 0)
                if u[0] is not None or u[1] + 2 < UNITS:
                    sp.wait_ge(norm, at(u, NORM, 1))
                    load_x(off(u, 2))
                if real_unit(off(u, 1)):
                    load_adj(off(u, 1), 1)
                if not first(u) and real_unit(off(u, 1)):
                    load_raw(off(u, 1))
                if not first(u):
                    sp.wait_ge(x1_ready, at(off(u, -1), 2, 2))
                    store_x1(off(u, -1))

            walk(sp, unit, 0, UNITS, 1, UNITS - 3)

            sp.wait_ge(x1_ready, 2 * UNITS)
            store_x1((None, UNITS - 1))
            def expert_of(t):
                return sp.value_load(tab_e[0:1, cut(number(t, NS))], min_val=0, max_val=E - 1)

            def row_of(t):
                return sp.value_load(tab_row[0:1, cut(number(t, NS))], min_val=0, max_val=DUMMY + TILE)

            def load_w(t, e, pack, buf, sems):
                s = t[1] % 2
                sp.dma_start(buf[s][:, :, :].rearrange("p a n -> p (a n)").bitcast(FP32),
                             pack[:, cut(e), :, :].rearrange("p o a n -> p (o a n)").bitcast(FP32)).then_inc(sems[s], 16)

            def load_rows(t, e, row):
                s = t[1] % NS
                sp.dma_start(xt[s][:, :, :].rearrange("p j c -> p (j c)"),
                             sorted_rows[bass.ds(row, TILE), :].rearrange("(p j) c -> p (j c)", j=J)).then_inc(xt_in[s], 16)
                sp.dma_start(bbuf[s][:, :], bpack[:, cut(e), :].rearrange("p o b -> p (o b)")).then_inc(xt_in[s], 16)

            sp.wait_ge(w_lo, 2 * UNITS)
            sp.wait_ge(b1_ready, UNITS)
            sp.wait_ge(rows_ready, (UT + 1) * (UNITS - 1))
            sp.wait_ge(table, TABLE)
            experts = []
            for b in range(EARLY):
                t = (None, b)
                row = row_of(t)
                late = sp.value_load(tab_late[0:1, b:b + 1], min_val=0, max_val=1)
                e = expert_of(t)
                if b == 0:
                    sp.wait_ge(scattered[0], UNITS // 2 * UT * K * 16)
                sp.wait_ge(scattered[1], late * (UT * K * 16) + (UNITS // 2 - 1) * UT * K * 16)
                sp.wait_ge(padding, late * (16 * E) + 32)
                load_rows(t, e, row)
                if b < 2:
                    load_w(t, e, w1pack, w1buf, w1_in)
                    experts.append(e)
                if b > 0:
                    load_w((None, b - 1), experts[b - 1], w2pack, w2buf, w2_in)
            sp.wait_ge(h_done, HC)
            load_w(t, e, w1pack, w1buf, w1_in)
            sp.wait_ge(scattered[1], UNITS // 2 * UT * K * 16)
            sp.wait_ge(padding, 16 * E + 32)

            def tile(t):
                if real_tile(off(t, 3)):
                    e3rd, row = expert_of(off(t, 3)), row_of(off(t, 3))
                    sp.wait_ge(h_done, tat(t, HC, 2 * HC))
                    load_w(off(t, 3), e3rd, w1pack, w1buf, w1_in)
                    if t[0] is not None or t[1] >= 3:
                        sp.wait_ge(ys_ready, tat(off(t, -3), 2, 2))
                    load_rows(off(t, 3), e3rd, row)
                if real_tile(off(t, 2)):
                    e2nd = expert_of(off(t, 2))
                    used_w2 = early(sp, tat(t, 1, 1))
                    sp.wait_ge(table, TABLE)
                    sp.wait_ge(y_done, used_w2)
                    load_w(off(t, 2), e2nd, w2pack, w2buf, w2_in)

            walk_tiles(sp, tile)


        @block.scalar
        def _(act):
            act.wait_ge(dve_const, 1)
            act.activation(warm[:, :], ones[:, 0:1], ACT.Exp).then_inc(table_in, 1)
            act.wait_ge(table_in, 1)
            act.activation(warm[:, :], ones[:, 0:1], ACT.Identity).then_inc(table_in, 1)
            act.wait_ge(table_in, 2)

            def norm_x(u, g):
                p = u[1] % 2
                ready = early(act, at(u, NORM, NORM))
                act.wait_ge(pool_const, 1)
                act.wait_ge(norm, ready)
                if not first(u):
                    used = early(act, at(off(u, -1), 2, g + 1))
                    act.wait_ge(pool_const, 1)
                    act.wait_ge(g_done, used)
                for q in range(Q):
                    t = g * Q + q
                    act.activation(xn[g][:, q, :], x_all[:, graph(u, g), q, :].rearrange("p o d -> p (o d)"), ACT.Identity,
                                   bias=shift[p][:, 1, t:t + 1], scale=rstd[p][:, 1, t:t + 1]).then_inc(xn_ready, 1)

            def norm_z(u, g):
                p = u[1] % 2
                ready = early(act, at(off(u, 2), NORM, NORM))
                act.wait_ge(pool_const, 1)
                act.wait_ge(norm, ready)
                if not first(u):
                    used = early(act, at(off(u, -1), 2, g + 1))
                    act.wait_ge(pool_const, 1)
                    act.wait_ge(z_turned, used)
                for q in range(Q):
                    t = g * Q + q
                    act.activation(z[g][:, q, :], x_all[:, graph(u, g), q, :].rearrange("p o d -> p (o d)"), ACT.Identity,
                                   bias=shift[p][:, 0, t:t + 1], scale=rstd[p][:, 0, t:t + 1]).then_inc(z_ready, 1)

            def copy_adjT(u, g, half):
                if not first(u) and half == 0:
                    act.wait_ge(g_done, at(off(u, -1), 2, g + 1))
                for r in (2 * half, 2 * half + 1):
                    act.wait_ge(adj_turned, at(u, UT, g * Q + r + 1))
                    act.activation(adjT[g][:, r, :], psT[r % 2][:, :], ACT.Copy).then_inc(adjT_ready, 1)

            def copy_gT(u, g):
                if not first(u):
                    act.wait_ge(w_done, at(off(u, -1), 2, g + 1))
                act.wait_ge(g_done, at(u, 2, g + 1))
                act.activation(gT[g][:, :], psG[:, :], ACT.Copy).then_inc(gT_ready, 1)

            def copy_zT(u, g):
                if not first(u):
                    act.wait_ge(l_done, at(off(u, -1), 2, g + 1))
                act.wait_ge(z_turned, at(u, 2, g + 1))
                act.activation(zT[g][:, :], psZ[:, :], ACT.Copy).then_inc(zT_ready, 1)

            def exp_gap(u):
                act.wait_ge(route, at(u, ROUTE, 9))
                act.activation(e2[:, :], gap[:, :], ACT.Exp).then_inc(exp_ready, 1)

            def weights_hi(u):
                s = u[1] % 2
                e = cut(number(u, 2))
                ready = early(act, unit_slot(u, 32))
                scale = gcol[:, e]
                act.wait_ge(vecT_ready, 1)
                act.wait_ge(raw_in[s], ready)
                if not first(u):
                    used = early(act, at(off(u, -1), 2, 2))
                    act.wait_ge(vecT_ready, 1)
                    act.wait_ge(w_lo, used)
                act.activation(w1g[:, :], w1raw[s][:, :], ACT.Identity, scale=scale).then_inc(w_hi, 1)
                act.activation(w1pack[:, e, 0, :].rearrange("p o h -> p (o h)"), w1raw[s][:, :], ACT.Identity, scale=scale)\
                    .then_inc(w_hi, 1)
                act.activation(w2pack[:, e, 0, :].rearrange("p o h -> p (o h)"),
                               w2raw[s][:, :, :].rearrange("p c d -> p (c d)"), ACT.Copy).then_inc(w_hi, 1)

            def unit(u):
                if real_unit(u):
                    if not first(u):
                        weights_hi(u)
                    copy_gT(u, 0)
                    copy_adjT(u, 1, 0)
                if real_unit(off(u, -2)):
                    exp_gap(off(u, -2))
                if real_unit(u):
                    copy_adjT(u, 1, 1)
                    if first(u):
                        weights_hi(u)
                if real_unit(off(u, -1)):
                    norm_z(off(u, -1), 0)
                    norm_z(off(u, -1), 1)
                if first(u):
                    norm_x(off(u, 1), 0)
                if real_unit(u):
                    copy_gT(u, 1)
                if real_unit(off(u, 1)):
                    copy_adjT(off(u, 1), 0, 0)
                if real_unit(off(u, -1)):
                    copy_zT(off(u, -1), 0)
                if real_unit(off(u, 1)):
                    copy_adjT(off(u, 1), 0, 1)
                if real_unit(off(u, 1)) and not first(u):
                    norm_x(off(u, 1), 0)
                if real_unit(off(u, -1)):
                    copy_zT(off(u, -1), 1)
                if real_unit(off(u, 1)):
                    norm_x(off(u, 1), 1)

            copy_adjT((None, 0), 0, 0)
            norm_x((None, 0), 0)
            copy_adjT((None, 0), 0, 1)
            norm_x((None, 0), 1)
            walk(act, unit, 0, UNITS + 2, 2, UNITS - 2)

            def gelu(t):
                s, p = t[1] % NS, t[1] % 2
                if t[0] is not None or t[1] >= 2:
                    act.wait_ge(y_done, tat(off(t, -1), 1))
                for c in range(HC):
                    if t[0] is not None or t[1] >= 1:
                        used = early(act, tat(off(t, -1), 6, (1, 2, 4, 6)[c]))
                        act.wait_ge(vecT_ready, 1)
                        act.wait_ge(h_split, used)
                    act.wait_ge(h_done, tat(t, HC, c + 1))
                    act.activation(h[:, c, :], psH[c][:, :], ACT.Gelu, bias=bbuf[s][:, c:c + 1]).then_inc(gelu_done, 1)
                    if 1 <= c <= 2:
                        act.wait_ge(gelu_done, tat(t, HC, c))
                        act.activation(h_hi[p][:, c - 1, :], h[:, c - 1, :], ACT.Copy).then_inc(hi_done, 1)

            def copy_yT(t):
                if t[0] is not None or t[1] >= 1:
                    act.wait_ge(y_turned, tat(t, 1))
                act.wait_ge(y_done, tat(t, 1, 1))
                act.activation(yT[:, :], psY[:, :], ACT.Identity, bias=bbuf[t[1] % NS][:, HC:HC + 1]).then_inc(yT_ready, 1)

            act.wait_ge(table, TABLE)
            for e in range(E):
                row = act.value_load(tab_pad[0:1, e:e + 1], min_val=0, max_val=DUMMY - TILE)
                act.dma_start(sorted_rows[bass.ds(row, TILE), :].rearrange("(p j) c -> p (j c)", j=J),
                              pad_tile[0][:, :, :].rearrange("p j c -> p (j c)")).then_inc(padding, 16)
            act.activation(warm[:, :], ones[:, 0:1], ACT.Gelu).then_inc(table_in, 1)
            gelu((None, 0))

            def tile(t):
                if real_tile(off(t, 1)):
                    gelu(off(t, 1))
                copy_yT(t)

            walk_tiles(act, tile)

        @block.tensor
        def _(pe):
            def turn_adj(u, g, half):
                pe.wait_ge(adj_loaded[g], at(u, 16, 16))
                for r in (2 * half, 2 * half + 1):
                    if not (first(u) and g == 0 and r < 2):
                        pe.wait_ge(adjT_ready, at(u, UT, g * Q + r - 1))
                    for q in range(Q):
                        last = nc.tensor.transpose(psT[r % 2][:, q * P:(q + 1) * P], adj_sb[g][:, q, r * P:(r + 1) * P], ident[:, :])
                    last.then_inc(adj_turned, 1)

            def aggregate(u, g):
                pe.wait_ge(xn_ready, at(u, UT, Q * (g + 1)))
                pe.wait_ge(adjT_ready, at(u, UT, Q * (g + 1)))
                if not (first(u) and g == 0):
                    pe.wait_ge(gT_ready, at(u, 2, g))
                for r in range(Q):
                    last = nc.tensor.matmul(psG[:, :], xn[g][:, r, :], adjT[g][:, r, :], start=(r == 0), stop=(r == Q - 1))
                last.then_inc(g_done, 1)

            def project(u, g):
                if first(u) and g == 0:
                    pe.wait_ge(small_loaded, SMALL)
                    pe.wait_ge(bias_split, 2)
                if not first(u):
                    pe.wait_ge(x1_ready, at(off(u, -1), 2, g + 1))
                nc.tensor.matmul(psO[g][:, :], ones_row[:, :], bias_hi[:, :], start=True, stop=False)
                nc.tensor.matmul(psO[g][:, :], ones_row[:, :], bias_lo[:, :], start=False, stop=False)
                pe.wait_ge(gT_ready, at(u, 2, g + 1))
                for q in range(Q):
                    last = nc.tensor.matmul(psO[g][:, q * D:(q + 1) * D], gT[g][:, q * P:(q + 1) * P], wg_sb[:, :],
                                            start=False, stop=(q == Q - 1))
                last.then_inc(w_done, 1)

            def turn_z(u, g):
                pe.wait_ge(z_ready, at(u, UT, Q * (g + 1)))
                if not (first(u) and g == 0):
                    pe.wait_ge(zT_ready, at(u, 2, g))
                for q in range(Q):
                    last = nc.tensor.transpose(psZ[:, q * P:(q + 1) * P], z[g][:, q, :], ident[:, :])
                last.then_inc(z_turned, 1)

            def logits(u, g):
                pe.wait_ge(zT_ready, at(u, 2, g + 1))
                if not first(u) and g == 0:
                    pe.wait_ge(route, at(off(u, -1), ROUTE, 1))
                for q in range(Q):
                    last = nc.tensor.matmul(psL[:, g * Q + q, :], zT[g][:, q * P:(q + 1) * P], wr_sb[:, :], start=True, stop=True)
                last.then_inc(l_done, 1)

            def shift_bias(u):
                s = u[1] % 2
                if first(u):
                    pe.wait_ge(vecT_ready, 1)
                pe.wait_ge(raw_in[s], unit_slot(u, 32))
                if not first(u):
                    pe.wait_ge(b1_ready, at(off(u, -1), 1, 1))
                for c in range(HC):
                    last = nc.tensor.matmul(psB1[:, c:c + 1], w1raw[s][:, c * P:(c + 1) * P], bcol[:, cut(number(u, 2))],
                                            start=True, stop=True)
                last.then_inc(b1_done, 1)

            def rank(u):
                pe.wait_ge(route, at(u, ROUTE, 14))
                if u[0] is None and u[1] == UNITS - 1:
                    nc.tensor.matmul(psEarly, ones[:, :], sel_before[:, :], start=True, stop=True)
                nc.tensor.matmul(psR[:, :, :], before[:, :], sel[:, :, :], start=True, stop=False)
                nc.tensor.matmul(psR[:, :, :], ones[:, :], sel_before[:, :].unsqueeze(1).to_broadcast([P, UT, E]), start=False, stop=False)
                for t in range(UT - 1):
                    last = nc.tensor.matmul(psR[:, t + 1:UT, :], ones[:, :],
                                            sel[:, t:t + 1, :].to_broadcast([P, UT - 1 - t, E]), start=False, stop=(t == UT - 2))
                last.then_inc(rank_done, 1)

            def unit(u):
                if real_unit(u):
                    aggregate(u, 0)
                    turn_adj(u, 1, 0)
                    shift_bias(u)
                if real_unit(off(u, -2)):
                    rank(off(u, -2))
                if real_unit(u):
                    turn_adj(u, 1, 1)
                    project(u, 0)
                    aggregate(u, 1)
                if real_unit(off(u, 1)):
                    turn_adj(off(u, 1), 0, 0)
                if real_unit(off(u, -1)):
                    turn_z(off(u, -1), 0)
                if real_unit(off(u, 1)):
                    turn_adj(off(u, 1), 0, 1)
                if real_unit(u):
                    project(u, 1)
                if real_unit(off(u, -1)):
                    turn_z(off(u, -1), 1)
                    logits(off(u, -1), 0)
                    logits(off(u, -1), 1)

            pe.wait_ge(pool_const, POOL_CONST)
            turn_adj((None, 0), 0, 0)
            turn_adj((None, 0), 0, 1)
            pe.wait_ge(vecs_loaded, VECS)
            nc.tensor.transpose(psVec, vecs[:, :], ident[0:VR, 0:VR]).then_inc(vecs_turned, 1)
            pe.wait_ge(dve_const, DVE_CONST)
            walk(pe, unit, 0, UNITS + 2, 2, UNITS - 2)
            pe.wait_ge(route, ROUTE * (UNITS - 1) + 20)
            pe.wait_ge(early_copied, 1)
            nc.tensor.matmul(psCnt, ones[:, :], sel_before[:, :], start=True, stop=True).then_inc(counted, 1)

            def turn_x(t):
                s = t[1] % NS
                pe.wait_ge(xt_in[s], by_slot(t, 32, NS))
                if t[0] is not None or t[1] >= 1:
                    pe.wait_ge(x_split, tat(t, 2))
                for i in range(J):
                    last = nc.tensor.transpose(psX[:, i * P:(i + 1) * P], xt[s][:, i, 0:D], ident[:, :])
                last.then_inc(xt_turned, 1)

            def up(t, chunks=range(HC)):
                p = t[1] % 2
                pe.wait_ge(w1_in[p], by_slot(t, 16, 2))
                pe.wait_ge(x_split, tat(t, 2, 2))
                for c in chunks:
                    if t[0] is not None or t[1] >= 1:
                        pe.wait_ge(gelu_done, tat(off(t, -1), HC, c + 1))
                    hi, lo = (w1buf[p][:, a, c * P:(c + 1) * P] for a in range(2))
                    nc.tensor.matmul(psH[c][:, :], hi, x_hi[p][:, :], start=True, stop=False)
                    nc.tensor.matmul(psH[c][:, :], hi, x_lo[p][:, :], start=False, stop=False)
                    nc.tensor.matmul(psH[c][:, :], lo, x_hi[p][:, :], start=False, stop=True).then_inc(h_done, 1)

            def down(t):
                p = t[1] % 2
                pe.wait_ge(w2_in[p], by_slot(t, 16, 2))
                if t[0] is not None or t[1] >= 1:
                    pe.wait_ge(yT_ready, tat(t, 1))
                for c in range(HC):
                    pe.wait_ge(h_split, tat(t, 6, (1, 2, 4, 6)[c]))
                    hi, lo = (w2buf[p][:, a, c * D:(c + 1) * D] for a in range(2))
                    nc.tensor.matmul(psY[:, :], hi, h_hi[p][:, c, :], start=(c == 0), stop=False)
                    nc.tensor.matmul(psY[:, :], hi, h_lo[p][:, c, :], start=False, stop=False)
                    last = nc.tensor.matmul(psY[:, :], lo, h_hi[p][:, c, :], start=False, stop=(c == HC - 1))
                last.then_inc(y_done, 1)

            def turn_y(t):
                pe.wait_ge(yT_ready, tat(t, 1, 1))
                if t[0] is not None or t[1] >= 1:
                    pe.wait_ge(ys_ready, tat(t, 2))
                for i in range(J):
                    last = nc.tensor.transpose(psYt[:, i * P:(i + 1) * P], yT[:, i * P:(i + 1) * P], ident[:, :])
                last.then_inc(y_turned, 1)

            pe.wait_ge(table, 2)
            turn_x((None, 0))
            up((None, 0), range(HC - 1))
            turn_x((None, 1))
            up((None, 0), [HC - 1])

            def tile(t):
                if t[0] is None and t[1] == 1:
                    turn_y((None, 0))
                if real_tile(off(t, 1)):
                    up(off(t, 1))
                if real_tile(off(t, 2)):
                    turn_x(off(t, 2))
                if t[0] is not None or t[1] >= 2:
                    turn_y(off(t, -1))
                down(t)

            walk_tiles(pe, tile)
            turn_y((None, TILES - 1))

        @block.vector
        def _(dve):
            V = nc.vector
            V.memset(ones[:, :], 1.0).then_inc(dve_const, 1)
            for k in range(2):
                V.memset(pad_tile[k][:, :, :], 0.0).then_inc(dve_const, 1)
            dve.wait_ge(dve_const, 1)
            V.tensor_copy(ones_row[:, :], ones[0:1, :]).then_inc(dve_const, 1)
            V.memset(sel_before[:, :], 0.0).then_inc(dve_const, 1)
            V.memset(one8[:, :], 1.0).then_inc(dve_const, 1)
            V.memset(stats[:, :, :, :], 1.0).then_inc(dve_const, 1)
            dve.wait_ge(pool_const, POOL_CONST)
            V.tensor_scalar(region_of[:, :], iota_i[:, 0:E], float(REGION), None, ALU.mult).then_inc(dve_const, 1)
            V.tensor_scalar(prefer_low[:, :], iota_i[:, 0:E], -1.0, float(E), ALU.mult, ALU.add).then_inc(dve_const, 1)
            V.tensor_scalar(thr[:, :], iota_i[0:1, 0:MAXT], float(TILE), None, ALU.mult).then_inc(dve_const, 1)
            V.tensor_copy(tnum[:, :], iota_i[0:1, 0:TILES]).then_inc(dve_const, 1)
            V.tensor_copy(dummy_row[:, :], dummy_i[:, 0:TILES]).then_inc(dve_const, 1)
            dve.wait_ge(dve_const, 12)
            V.scalar_tensor_tensor(row_less[:, :], tnum[:, :], float(TILE), dummy_row[:, :], ALU.mult, ALU.subtract).then_inc(dve_const, 1)
            V.tensor_copy(last_land[:, :], land_i[:, 1:TILES + 1]).then_inc(dve_const, 1)
            V.memset(same[:, :], 0.0).then_inc(dve_const, 1)
            dve.wait_ge(dve_const, DVE_CONST)

            def stats_of_x(n):
                p = n[1] % 2
                dve.wait_ge(x_in[p], unit_slot(n, 16))
                if n[0] is not None or n[1] >= 1:
                    seen = early(dve, at(off(n, -1), NORM, NORM))
                    dve.wait_ge(dve_const, DVE_CONST)
                    dve.wait_ge(norm, seen)
                for t in range(UT):
                    V.bn_stats(stats[:, 1, t, :], x_all[:, graph(n, t // Q), t % Q, :].rearrange("p o d -> p (o d)"))\
                        .then_inc(stats_x, 1)

            def stats_of_x1(u):
                both_in = early(dve, at(u, 2, 2))
                dve.wait_ge(dve_const, DVE_CONST)
                dve.wait_ge(x1_ready, both_in)
                for t in range(UT):
                    V.bn_stats(stats[:, 0, t, :], x_all[:, graph(u, t // Q), t % Q, :].rearrange("p o d -> p (o d)"))\
                        .then_inc(stats_x1, 1)

            def per_tile(ap):
                return ap[:, :].unsqueeze(2).to_broadcast([P, UT, E])

            def per_expert(ap):
                return ap[:, :].unsqueeze(1).to_broadcast([P, UT, E])

            def norms_and_choice(n, norms, choice):
                p = n[1] % 2
                u = off(n, -3)
                r = lambda k: at(n, NORM, k)
                c = lambda k: at(u, ROUTE, k)
                if norms:
                    if real_unit(off(n, -2)):
                        dve.wait_ge(stats_x1, at(off(n, -2), UT, UT))
                    if real_unit(n):
                        dve.wait_ge(stats_x, at(n, UT, UT))
                    V.tensor_tensor(dif[:, :, :], stats[:, :, :, 1], stats[:, :, :, 4], ALU.subtract).then_inc(norm, 1)
                    V.tensor_tensor(spr[:, :, :], stats[:, :, :, 2], stats[:, :, :, 5], ALU.add).then_inc(norm, 1)
                    V.tensor_tensor(tot[:, :, :], stats[:, :, :, 1], stats[:, :, :, 4], ALU.add).then_inc(norm, 1)
                if choice:
                    dve.wait_ge(l_done, at(u, 2, 2))
                    V.tensor_tensor(lg[:, :, :], psL[:, :, :], per_expert(br_sb), ALU.add).then_inc(route, 1)
                if norms:
                    dve.wait_ge(norm, r(1))
                    V.scalar_tensor_tensor(sq[:, :, :], dif[:, :, :], 0.25, dif[:, :, :], ALU.mult, ALU.mult).then_inc(norm, 1)
                if choice:
                    dve.wait_ge(route, c(1))
                    V.tensor_reduce(top1[:, :], lg[:, :, :], AX.X, ALU.max).then_inc(route, 1)
                if norms:
                    dve.wait_ge(norm, r(4))
                    V.scalar_tensor_tensor(var[:, :, :], spr[:, :, :], 1.0 / D, sq[:, :, :], ALU.mult, ALU.add).then_inc(norm, 1)
                if choice:
                    dve.wait_ge(route, c(2))
                    V.tensor_tensor(eq1[:, :, :], lg[:, :, :], per_tile(top1), ALU.is_equal).then_inc(route, 1)
                if norms:
                    dve.wait_ge(norm, r(5))
                    V.tensor_scalar(arg[:, 0:2, :], var[:, :, :], LN_EPS, None, ALU.add).then_inc(norm, 1)
                if choice:
                    dve.wait_ge(route, c(3))
                    V.tensor_tensor(kk1[:, :, :], eq1[:, :, :], per_expert(prefer_low), ALU.mult).then_inc(route, 1)
                if norms:
                    dve.wait_ge(norm, r(6))
                    V.scalar_tensor_tensor(arg[:, 2, :], arg[:, 0, :], LN_EPS, var[:, 0, :], ALU.mult, ALU.add).then_inc(norm, 1)
                if choice:
                    dve.wait_ge(route, c(4))
                    V.tensor_reduce(key1[:, :], kk1[:, :, :], AX.X, ALU.max).then_inc(route, 1)
                if norms:
                    dve.wait_ge(norm, r(7))
                    V.tensor_scalar(half_bits[:, :, :], arg[:, :, :].bitcast(I32), 1, None, ALU.logical_shift_right).then_inc(norm, 1)
                if choice:
                    dve.wait_ge(route, c(5))
                    V.tensor_tensor(onehot[:, 0, :, :], kk1[:, :, :], per_tile(key1), ALU.is_equal).then_inc(route, 1)
                if norms:
                    dve.wait_ge(norm, r(8))
                    V.tensor_scalar(guess[:, :, :].bitcast(I32), half_bits[:, :, :], -1.0, float(MAGIC), ALU.mult, ALU.add).then_inc(norm, 1)
                if choice:
                    dve.wait_ge(route, c(6))
                    V.scalar_tensor_tensor(lg2[:, :, :], onehot[:, 0, :, :], -BIG, lg[:, :, :], ALU.mult, ALU.add).then_inc(route, 1)
                if norms:
                    dve.wait_ge(norm, r(9))
                    V.tensor_tensor(newton_a[:, :, :], arg[:, :, :], guess[:, :, :], ALU.mult).then_inc(norm, 1)
                if choice:
                    dve.wait_ge(route, c(7))
                    V.tensor_reduce(top2[:, :], lg2[:, :, :], AX.X, ALU.max).then_inc(route, 1)
                if norms:
                    dve.wait_ge(norm, r(10))
                    V.scalar_tensor_tensor(newton_b[:, :, :], newton_a[:, :, :], -0.5, guess[:, :, :], ALU.mult, ALU.mult).then_inc(norm, 1)
                if choice:
                    dve.wait_ge(route, c(8))
                    V.tensor_tensor(gap[:, :], top2[:, :], top1[:, :], ALU.subtract).then_inc(route, 1)
                    V.tensor_tensor(eq2[:, :, :], lg2[:, :, :], per_tile(top2), ALU.is_equal).then_inc(route, 1)
                if norms:
                    dve.wait_ge(norm, r(11))
                    V.scalar_tensor_tensor(guess[:, :, :], newton_b[:, :, :], 1.5, guess[:, :, :], ALU.add, ALU.mult).then_inc(norm, 1)
                if choice:
                    dve.wait_ge(route, c(10))
                    V.tensor_tensor(kk2[:, :, :], eq2[:, :, :], per_expert(prefer_low), ALU.mult).then_inc(route, 1)
                if norms:
                    dve.wait_ge(norm, r(12))
                    V.tensor_tensor(newton_a[:, :, :], arg[:, :, :], guess[:, :, :], ALU.mult).then_inc(norm, 1)
                if choice:
                    dve.wait_ge(route, c(11))
                    V.tensor_reduce(key2[:, :], kk2[:, :, :], AX.X, ALU.max).then_inc(route, 1)
                if norms:
                    dve.wait_ge(norm, r(13))
                    V.scalar_tensor_tensor(newton_b[:, :, :], newton_a[:, :, :], -0.5, guess[:, :, :], ALU.mult, ALU.mult).then_inc(norm, 1)
                if choice:
                    dve.wait_ge(route, c(12))
                    V.tensor_tensor(onehot[:, 1, :, :], kk2[:, :, :], per_tile(key2), ALU.is_equal).then_inc(route, 1)
                if norms:
                    dve.wait_ge(norm, r(14))
                    V.scalar_tensor_tensor(guess[:, :, :], newton_b[:, :, :], 1.5, guess[:, :, :], ALU.add, ALU.mult).then_inc(norm, 1)
                if choice:
                    dve.wait_ge(route, c(13))
                    V.tensor_tensor(sel[:, :, :], onehot[:, 0, :, :], onehot[:, 1, :, :], ALU.add).then_inc(route, 1)
                if norms:
                    dve.wait_ge(norm, r(15))
                    V.tensor_tensor(newton_a[:, :, :], arg[:, :, :], guess[:, :, :], ALU.mult).then_inc(norm, 1)
                if norms:
                    dve.wait_ge(norm, r(16))
                    V.scalar_tensor_tensor(newton_b[:, :, :], newton_a[:, :, :], -0.5, guess[:, :, :], ALU.mult, ALU.mult).then_inc(norm, 1)
                if norms:
                    dve.wait_ge(norm, r(17))
                    V.scalar_tensor_tensor(rstd[p][:, :, :], newton_b[:, :, :], 1.5, guess[:, :, :], ALU.add, ALU.mult).then_inc(norm, 1)
                if norms:
                    V.tensor_scalar(mean2[p][:, :], tot[:, 0, :], 0.5, None, ALU.mult).then_inc(norm, 1)
                    dve.wait_ge(norm, r(18))
                    V.scalar_tensor_tensor(shift[p][:, :, :], tot[:, :, :], -0.5, rstd[p][:, 0:2, :], ALU.mult, ALU.mult).then_inc(norm, 1)

            def residual(u, g):
                dve.wait_ge(w_done, at(u, 2, g + 1))
                xs = x_all[:, graph(u, g), :, :].rearrange("p o q d -> p (o q d)")
                V.tensor_tensor(xs, psO[g][:, :], xs, ALU.add).then_inc(x1_ready, 1)

            def make_rows(u):
                p = u[1] % 2
                dve.wait_ge(norm, at(off(u, 2), NORM, NORM - 1))
                dve.wait_ge(rows_free, at(u, 1, 1))
                for t in range(UT):
                    V.tensor_scalar(rows[p][:, t, :, 0:D], x_all[:, graph(u, t // Q), t % Q, :].to_broadcast([P, K, D]),
                                    mean2[p][:, t:t + 1], rstd[p][:, 2, t:t + 1], ALU.subtract, ALU.mult).then_inc(rows_ready, 1)
                idx = rows[p][:, :, :, D:D + 1].bitcast(I32)
                V.tensor_scalar(idx, idx, 4.0 * N, None, ALU.add).then_inc(rows_ready, 1)

            def assign(u):
                p = u[1] % 2
                r = lambda k: at(u, ROUTE, k)
                dve.wait_ge(exp_ready, at(u, 1, 1))
                V.tensor_scalar(den[:, :], e2[:, :], 1.0, None, ALU.add).then_inc(route, 1)
                dve.wait_ge(route, r(15))
                dve.wait_ge(rows_free, at(u, 1, 1))
                V.reciprocal(rows[p][:, :, 0, D + 1], den[:, :]).then_inc(route, 1)
                dve.wait_ge(route, r(16))
                V.tensor_tensor(rows[p][:, :, 1, D + 1], rows[p][:, :, 0, D + 1], e2[:, :], ALU.mult).then_inc(route, 1)
                dve.wait_ge(rank_done, at(u, 1, 1))
                V.tensor_tensor(pos[:, :, :], psR[:, :, :], per_expert(region_of), ALU.add).then_inc(route, 1)
                V.tensor_reduce(sel_sum[:, :], sel[:, :, :].rearrange("p t e -> p e t"), AX.X, ALU.add).then_inc(route, 1)
                if u[0] is None and u[1] == UNITS - 1:
                    V.tensor_copy(cnt_early[:, :], psEarly[0:1, :]).then_inc(early_copied, 1)
                dve.wait_ge(route, r(19))
                V.tensor_tensor(sel_before[:, :], sel_before[:, :], sel_sum[:, :], ALU.add).then_inc(route, 1)
                for k in range(K):
                    V.tensor_tensor(place[:, k, :, :], onehot[:, k, :, :], pos[:, :, :], ALU.mult).then_inc(route, 1)
                dve.wait_ge(route, r(22))
                with nc.allow_low_precision(reason="a sum of one whole number below 2^24 and zeros"):
                    V.tensor_reduce(slot[p][:, :, :], place[:, :, :, :], AX.X, ALU.add).then_inc(route, 1)

            def weights_lo(u):
                s = u[1] % 2
                e = cut(number(u, 2))
                dve.wait_ge(w_hi, at(u, 3, 3))
                V.tensor_tensor(w1pack[:, e, 1, :].rearrange("p o h -> p (o h)"), w1g[:, :],
                                w1pack[:, e, 0, :].rearrange("p o h -> p (o h)").bitcast(FP32), ALU.subtract).then_inc(w_lo, 1)
                V.tensor_tensor(w2pack[:, e, 1, :].rearrange("p o h -> p (o h)"), w2raw[s][:, :, :].rearrange("p c d -> p (c d)"),
                                w2pack[:, e, 0, :].rearrange("p o h -> p (o h)").bitcast(FP32), ALU.subtract).then_inc(w_lo, 1)

            def fold_bias(u):
                dve.wait_ge(b1_done, at(u, 1, 1))
                V.tensor_tensor(bpack[:, cut(number(u, 2)), 0:HC].rearrange("p o c -> p (o c)"), psB1,
                                vecT[:, cut(number(u, 2, HC), HC)], ALU.add).then_inc(b1_ready, 1)

            def unit(u):
                if real_unit(off(u, -1)):
                    residual(off(u, -1), 1)
                    stats_of_x1(off(u, -1))
                norms_and_choice(off(u, 1), u[0] is not None or u[1] <= UNITS, real_unit(off(u, -2)))
                if real_unit(off(u, -2)):
                    assign(off(u, -2))
                if real_unit(u):
                    residual(u, 0)
                    weights_lo(u)
                    fold_bias(u)
                if u[0] is not None or u[1] + 2 < UNITS:
                    stats_of_x(off(u, 2))
                if u[0] is not None or 1 <= u[1] < UNITS:
                    make_rows(off(u, -1))

            stats_of_x((None, 0))
            norms_and_choice((None, 0), True, False)
            stats_of_x((None, 1))
            dve.wait_ge(small_loaded, SMALL)
            V.tensor_copy(bias_hi[:, :], bias_row[:, :]).then_inc(bias_split, 1)
            dve.wait_ge(bias_split, 1)
            V.tensor_tensor(bias_lo[:, :], bias_row[:, :], bias_hi[:, :].bitcast(FP32), ALU.subtract).then_inc(bias_split, 1)
            dve.wait_ge(vecs_turned, 1)
            V.tensor_copy(vecT[:, :], psVec).then_inc(vecT_ready, 1)
            dve.wait_ge(vecT_ready, 1)
            V.tensor_copy(bpack[:, :, HC], b2col).then_inc(vecT_ready, 1)
            walk(dve, unit, 0, UNITS + 2, 2, UNITS - 2)

            n = [0]

            def step(ins):
                n[0] += 1
                ins.then_inc(table, 1)
                dve.wait_ge(table, n[0])

            def beside(ins):
                n[0] += 1
                ins.then_inc(table, 1)

            te = [1, TILES, E]
            dve.wait_ge(counted, 1)
            dve.wait_ge(early_copied, 1)
            step(V.tensor_copy(cnt[:, :], psCnt[0:1, :]))
            beside(V.tensor_tensor(base_row[:, :], cnt[:, :], region_of[0:1, :], ALU.add))
            beside(V.tensor_tensor(early_end[:, :], cnt_early[:, :], region_of[0:1, :], ALU.add))
            step(V.tensor_tensor(more[:, :, :], cnt[:, :].unsqueeze(2).to_broadcast([1, E, MAXT]),
                                 thr[:, :].unsqueeze(1).to_broadcast([1, E, MAXT]), ALU.is_gt))
            beside(V.tensor_copy(tab_pad[:, :], base_row[:, :]))
            step(V.tensor_reduce(nt[:, :], more[:, :, :], AX.X, ALU.add))
            step(V.tensor_tensor_scan(t_end[:, :], one8[:, :], nt[:, :], 0.0, ALU.mult, ALU.add))
            beside(V.tensor_tensor(ge_end[:, :, :], tnum[:, :].unsqueeze(2).to_broadcast(te), t_end[:, :].unsqueeze(1).to_broadcast(te), ALU.is_ge))
            step(V.tensor_tensor(t_start[:, :], t_end[:, :], nt[:, :], ALU.subtract))
            beside(V.scalar_tensor_tensor(row_start[:, :], t_start[:, :], float(-TILE), region_of[0:1, :], ALU.mult, ALU.add))
            step(V.tensor_tensor(ge_start[:, :, :], tnum[:, :].unsqueeze(2).to_broadcast(te), t_start[:, :].unsqueeze(1).to_broadcast(te), ALU.is_ge))
            beside(V.tensor_reduce(eid[:, :], ge_end[:, :, :], AX.X, ALU.add))
            step(V.tensor_tensor(mine[:, :, :], ge_start[:, :, :], ge_end[:, :, :], ALU.subtract))
            beside(V.tensor_scalar(tab_e[:, :], eid[:, :], float(E - 1), None, ALU.min))
            beside(V.tensor_reduce(real[:, :], mine[:, :, :], AX.X, ALU.add))
            beside(V.tensor_tensor(mine_early[:, :, :], mine[:, 0:EARLY, :], early_end[:, :].unsqueeze(1).to_broadcast([1, EARLY, E]), ALU.mult))
            step(V.tensor_tensor(mine_row[:, :, :], mine[:, :, :], row_start[:, :].unsqueeze(1).to_broadcast(te), ALU.mult))
            beside(V.tensor_reduce(tile_early[:, :], mine_early[:, :, :], AX.X, ALU.add))
            beside(V.tensor_tensor(row_b[:, :], real[:, :], row_less[:, :], ALU.mult))
            beside(V.tensor_tensor(same[:, 1:TILES], eid[:, 1:TILES], eid[:, 0:TILES - 1], ALU.is_equal))
            step(V.tensor_reduce(row_a[:, :], mine_row[:, :, :], AX.X, ALU.add))
            beside(V.scalar_tensor_tensor(tab_land[:, :], same[:, :], float(-J * 16), last_land[:, :], ALU.mult, ALU.add))
            step(V.tensor_tensor(row_c[:, :], row_a[:, :], row_b[:, :], ALU.add))
            step(V.tensor_tensor(row_d[:, :], row_c[:, :], dummy_row[:, :], ALU.add))
            beside(V.tensor_copy(tab_row[:, :], row_d[:, :]))
            step(V.scalar_tensor_tensor(tab_late[:, :], row_d[:, 0:EARLY], float(TILE), tile_early[:, :], ALU.add, ALU.is_gt))
            make_rows((None, UNITS - 1))

            def split_x(t):
                p = t[1] % 2
                if t[0] is not None or t[1] >= 2:
                    dve.wait_ge(h_done, tat(off(t, -1), HC))
                dve.wait_ge(xt_turned, tat(t, 1, 1))
                V.tensor_copy(x_hi[p][:, :], psX[:, :]).then_inc(x_split, 1)
                dve.wait_ge(x_split, tat(t, 2, 1))
                V.tensor_tensor(x_lo[p][:, :], psX[:, :], x_hi[p][:, :].bitcast(FP32), ALU.subtract).then_inc(x_split, 1)

            def split_h(t, c):
                p = t[1] % 2
                if c == 0 and (t[0] is not None or t[1] >= 2):
                    dve.wait_ge(y_done, tat(off(t, -1), 1))
                if c < 2:
                    dve.wait_ge(hi_done, tat(t, 2, c + 1))
                else:
                    dve.wait_ge(gelu_done, tat(t, HC, c + 1))
                    V.tensor_copy(h_hi[p][:, c, :], h[:, c, :]).then_inc(h_split, 1)
                    dve.wait_ge(h_split, tat(t, 6, (3, 5)[c - 2]))
                V.tensor_tensor(h_lo[p][:, c, :], h[:, c, :], h_hi[p][:, c, :].bitcast(FP32), ALU.subtract).then_inc(h_split, 1)

            def finish(t):
                s, p = t[1] % NS, t[1] % 2
                if t[0] is not None or t[1] >= 2:
                    dve.wait_ge(y_scattered[p], by_slot(off(t, -2), J * 16, 2))
                V.tensor_copy(result_row[p][:, :], xt[s][:, :, D:D + 1].bitcast(I32).rearrange("p j o -> p (j o)"))\
                    .then_inc(ys_ready, 1)
                dve.wait_ge(y_turned, tat(t, 1, 1))
                V.tensor_tensor(ys[p][:, :, :], psYt[:, :].rearrange("p (j d) -> p j d", j=J),
                                xt[s][:, :, D + 1:D + 2].to_broadcast([P, J, D]), ALU.mult).then_inc(ys_ready, 1)

            split_x((None, 0))
            split_x((None, 1))
            for c in range(HC):
                split_h((None, 0), c)

            def tile(t):
                if real_tile(off(t, 1)):
                    split_h(off(t, 1), 0)
                if real_tile(off(t, 2)):
                    split_x(off(t, 2))
                if real_tile(off(t, 1)):
                    split_h(off(t, 1), 1)
                if t[0] is not None or t[1] >= 1:
                    finish(off(t, -1))
                if real_tile(off(t, 1)):
                    split_h(off(t, 1), 2)
                    split_h(off(t, 1), 3)

            walk_tiles(dve, tile)
            finish((None, TILES - 1))

        @block.gpsimd
        def _(pool):
            G = nc.gpsimd
            G.memset(ident[:, :], 0.0).then_inc(pool_const, 1)
            G.memset(before[:, :], 0.0).then_inc(pool_const, 1)
            pool.wait_ge(pool_const, 2)
            G.affine_select(out=ident[:, :], in_=ident[:, :], compare_op=ALU.not_equal, fill=1.0, base=0,
                            pattern=[[-1, P]], channel_multiplier=1).then_inc(pool_const, 1)
            G.affine_select(out=before[:, :], in_=before[:, :], compare_op=ALU.is_ge, fill=1.0, base=0,
                            pattern=[[-1, P]], channel_multiplier=1).then_inc(pool_const, 1)
            G.iota(iota_i[:, :], pattern=[[1, 64]], base=0, channel_multiplier=0).then_inc(pool_const, 1)
            for u in range(2):
                idx = rows[u][:, :, :, D:D + 1].bitcast(I32).rearrange("p t k o -> p t (k o)")
                G.iota(idx, pattern=[[P, UT], [0, K]], base=2 * N * (u - 2), channel_multiplier=1).then_inc(pool_const, 1)
            G.iota(land_i[:, :], pattern=[[J * 16, TILES // 2 + 1], [0, 2]], base=0, channel_multiplier=0).then_inc(pool_const, 1)
            G.iota(dummy_i[:, :], pattern=[[0, TILES // 2 + 1], [TILE, 2]], base=DUMMY, channel_multiplier=0).then_inc(pool_const, 1)
            pool.wait_ge(dve_const, 4)
            for k in range(2):
                G.iota(pad_tile[k][:, :, D:D + 1].bitcast(I32).rearrange("p j o -> p (j o)"), pattern=[[1, J]],
                       base=TOK + k * TILE, channel_multiplier=J).then_inc(pool_const, 1)
            pool.sem_inc(rows_free, 2)

            def scatter(u):
                p = u[1] % 2
                slots_in = early(pool, at(u, ROUTE, 23))
                rows_in = early(pool, at(u, UT + 1, UT + 1))
                pool.wait_ge(pool_const, POOL_CONST)
                pool.wait_ge(route, slots_in)
                pool.wait_ge(rows_ready, rows_in)
                for t in range(UT):
                    for k in range(K):
                        G.indirect_dma_start(out=sorted_rows, out_offset=bass.IndirectOffsetOnAxis(ap=slot[p][:, k, t:t + 1], axis=0),
                                             in_=rows[p][:, t, k, :], in_offset=None,
                                             bounds_check=DUMMY - 1, oob_is_err=False).then_inc(scattered[p], 16)
                    if t == 1 and (u[0] is not None or u[1] >= 1):
                        pool.wait_ge(scattered[1 - p], unit_slot(off(u, -1), UT * K * 16))
                        pool.sem_inc(rows_free, 1)

            scatter((None, 0))
            with pool.Fori(0, UNITS // 2 - 1) as j:
                scatter((j, 1))
                scatter((j, 2))
            scatter((None, UNITS - 1))

            def send(t):
                p = t[1] % 2
                both_in = early(pool, tat(t, 2, 2))
                if t[0] is not None or t[1] >= 3:
                    landed = pool.value_load(tab_land[0:1, cut(number(t, NS))], min_val=J * 16, max_val=TILES * J * 16)
                elif t[1] >= 1:
                    landed = by_slot(off(t, -1), J * 16, 2)
                pool.wait_ge(pool_const, POOL_CONST)
                pool.wait_ge(ys_ready, both_in)
                if t[0] is not None or t[1] >= 1:
                    pool.wait_ge(y_scattered[1 - p], landed)
                for i in range(J):
                    G.indirect_dma_start(out=out,
                                         out_offset=bass.IndirectOffsetOnAxis(ap=result_row[p][:, i:i + 1], axis=0),
                                         in_=ys[p][:, i, :], in_offset=None, compute_op=ALU.add).then_inc(y_scattered[p], 16)

            pool.wait_ge(table, TABLE)
            pool.wait_ge(x1_stored, 16 * UNITS)
            pool.wait_ge(zeros_stored, 32)
            walk_tiles(pool, send)
            for s in range(2):
                pool.wait_ge(y_scattered[s], (TILES + 1 - s) // 2 * J * 16)


_INS = ['x', 'adj', 'L0_gnn_weight', 'L0_gnn_bias', 'L0_ffn_Wr', 'L0_ffn_br', 'L0_ffn_ln_g', 'L0_ffn_ln_b',
        'L0_ffn_W1', 'L0_ffn_b1', 'L0_ffn_W2', 'L0_ffn_b2']


def kernel(**inputs):
    import numpy as _np
    import concourse.bacc as _bacc
    from concourse import mybir as _mybir
    from concourse.bass_utils import run_bass_kernel_spmd as _run

    nc = _bacc.Bacc("TRN2", target_bir_lowering=False, num_devices=1)
    arrays, args = {}, []
    for name in _INS:
        a = _np.ascontiguousarray(inputs[name])
        arrays[f"in_{name}_dram"] = a
        args.append(nc.dram_tensor(f"in_{name}_dram", a.shape, _mybir.dt.from_np(a.dtype), kind="ExternalInput").ap())
    B, N, D = inputs["x"].shape
    out = nc.dram_tensor("out_dram", [B * N + 2 * TILE, D], _mybir.dt.float32, kind="ExternalOutput").ap()
    build(nc, *args, out)
    r = _run(nc, [arrays], core_ids=[0])
    return r.results[0]["out_dram"][0:B * N].reshape(B, N, D)
```
